# Optimizing a Trainium2 kernel written in Bass

```python
import numpy as np
import jax
import jax.numpy as jnp

def _softmax(x, axis=-1):
    return jax.nn.softmax(x, axis=axis)

def _gelu(x):
    return jax.nn.gelu(x, approximate=True)

def _silu(x):
    return jax.nn.silu(x)

def _sigmoid(x):
    return jax.nn.sigmoid(x)

def _layernorm(x, axis=-1, eps=1e-05):
    m = jnp.mean(x, axis=axis, keepdims=True)
    v = jnp.var(x, axis=axis, keepdims=True)
    return (x - m) / jnp.sqrt(v + eps)

def _scatter_add(tgt, idx, src, axis=0):
    return tgt.at[idx].add(src)

def _segment_sum(src, seg, n):
    return jax.ops.segment_sum(src, seg, n)
kernel_name = 'mk_hybrid_d1_jaxref_r8_a91dd8'

def setup_inputs(seed: int=0):
    np.random.seed(seed)
    _w = jnp.asarray

    def _L0_attn_a_setup():
        import jax, jax.numpy as jnp
        import numpy as np
        import math
        HIDDEN = 128
        NUM_LAYERS = 24
        INIT_RANGE = 0.02
        key = jax.random.key(seed)
        k1, k2 = jax.random.split(key)
        B, S, H = (4, 512, HIDDEN)
        hidden_states = jax.random.normal(k1, (B, S, H), dtype=jnp.float32)
        std = INIT_RANGE / math.sqrt(2.0 * NUM_LAYERS * H)
        W_q = jax.random.normal(k2, (H, H), dtype=jnp.float32) * std
        return {'hidden_states': hidden_states, 'W_q': W_q}
    _L0_attn_a_in = _L0_attn_a_setup()

    def _L0_attn_b_setup():
        import jax, jax.numpy as jnp
        import numpy as np
        B, T, C = (8, 256, 128)
        NL, LID = (12, 1)
        H = 4 * C

        def _ln(x, g, b):
            m = x.mean(-1, keepdims=True)
            v = ((x - m) ** 2).mean(-1, keepdims=True)
            return (x - m) * jax.lax.rsqrt(v + 1e-05) * g + b

        def _shift(x):
            return jnp.pad(x, ((0, 0), (1, 0), (0, 0)))[:, :-1]

        def _wkv(time_decay, time_first, k, v):
            w = -jnp.exp(time_decay)
            kt = jnp.moveaxis(k, 1, 0)
            vt = jnp.moveaxis(v, 1, 0)
            Bb, Cc = (k.shape[0], k.shape[2])
            init = (jnp.zeros((Bb, Cc), k.dtype), jnp.zeros((Bb, Cc), k.dtype), jnp.full((Bb, Cc), -1e+38, k.dtype))

            def step(carry, kv_t):
                aa, bb, pp = carry
                kk, vv = kv_t
                ww = time_first + kk
                p = jnp.maximum(pp, ww)
                e1 = jnp.exp(pp - p)
                e2 = jnp.exp(ww - p)
                out = (e1 * aa + e2 * vv) / (e1 * bb + e2)
                ww2 = pp + w
                p2 = jnp.maximum(ww2, kk)
                e1b = jnp.exp(ww2 - p2)
                e2b = jnp.exp(kk - p2)
                return ((e1b * aa + e2b * vv, e1b * bb + e2b, p2), out)
            _, out = jax.lax.scan(step, init, (kt, vt))
            return jnp.moveaxis(out, 0, 1)
        key = jax.random.key(seed)
        ks = jax.random.split(key, 8)
        f = lambda i, shape: 0.02 * jax.random.normal(ks[i], shape, jnp.float32)
        r01 = LID / (NL - 1)
        r10 = 1.0 - LID / NL
        h = np.arange(C, dtype=np.float64)
        decay = (-5 + 8 * (h / (C - 1)) ** (0.7 + 1.3 * r01)).astype(np.float32)
        zig = np.array([(i + 1) % 3 - 1 for i in range(C)]) * 0.5
        tfirst = (np.ones(C) * np.log(0.3) + zig).astype(np.float32)
        xpos = h / C
        tmk = (xpos ** r10).astype(np.float32)
        tmv = (xpos ** r10 + 0.3 * r01).astype(np.float32)
        tmr = (xpos ** (0.5 * r10)).astype(np.float32)
        cm = (xpos ** r10).astype(np.float32)
        return dict(x=jax.random.normal(ks[0], (B, T, C), jnp.float32), ln1_g=jnp.ones(C, jnp.float32), ln1_b=jnp.zeros(C, jnp.float32), ln2_g=jnp.ones(C, jnp.float32), ln2_b=jnp.zeros(C, jnp.float32), time_decay=jnp.asarray(decay), time_first=jnp.asarray(tfirst), time_mix_k=jnp.asarray(tmk), time_mix_v=jnp.asarray(tmv), time_mix_r=jnp.asarray(tmr), att_Wk=f(1, (C, C)), att_Wv=f(2, (C, C)), att_Wr=f(3, (C, C)), att_Wo=f(4, (C, C)), cm_k=jnp.asarray(cm), cm_r=jnp.asarray(cm), ffn_Wk=f(5, (H, C)), ffn_Wr=f(6, (C, C)), ffn_Wv=f(7, (C, H)))
    _L0_attn_b_in = _L0_attn_b_setup()

    def _L0_ffn_setup():
        import jax, jax.numpy as jnp
        import numpy as np
        B, S, D, F, E = (2, 256, 128, 512, 8)
        LN_EPS = 1e-05

        def _xavier(key, shape, fan_in, fan_out):
            a = np.sqrt(6.0 / (fan_in + fan_out))
            return jax.random.uniform(key, shape, jnp.float32, -a, a)
        key = jax.random.key(seed)
        ks = jax.random.split(key, 8)
        tgt = jax.random.normal(ks[0], (B, S, D), jnp.float32)
        router_w = _xavier(ks[1], (E, D), D, E)
        router_b = jnp.zeros((E,), jnp.float32)
        w1 = _xavier(ks[2], (E, D, F), D, F)
        b1 = jnp.zeros((E, F), jnp.float32)
        w2 = _xavier(ks[3], (E, F, D), F, D)
        b2 = jnp.zeros((E, D), jnp.float32)
        gamma = jnp.ones((D,), jnp.float32)
        beta = jnp.zeros((D,), jnp.float32)
        return {'tgt': tgt, 'router_w': router_w, 'router_b': router_b, 'w1': w1, 'b1': b1, 'w2': w2, 'b2': b2, 'gamma': gamma, 'beta': beta}
    _L0_ffn_in = _L0_ffn_setup()
    _d = {'L0_attn_a_hidden_states': _L0_attn_a_in['hidden_states'], 'L0_attn_a_W_q': _L0_attn_a_in['W_q'], 'L0_attn_b_ln1_g': _L0_attn_b_in['ln1_g'], 'L0_attn_b_ln1_b': _L0_attn_b_in['ln1_b'], 'L0_attn_b_ln2_g': _L0_attn_b_in['ln2_g'], 'L0_attn_b_ln2_b': _L0_attn_b_in['ln2_b'], 'L0_attn_b_time_decay': _L0_attn_b_in['time_decay'], 'L0_attn_b_time_first': _L0_attn_b_in['time_first'], 'L0_attn_b_time_mix_k': _L0_attn_b_in['time_mix_k'], 'L0_attn_b_time_mix_v': _L0_attn_b_in['time_mix_v'], 'L0_attn_b_time_mix_r': _L0_attn_b_in['time_mix_r'], 'L0_attn_b_att_Wk': _L0_attn_b_in['att_Wk'], 'L0_attn_b_att_Wv': _L0_attn_b_in['att_Wv'], 'L0_attn_b_att_Wr': _L0_attn_b_in['att_Wr'], 'L0_attn_b_att_Wo': _L0_attn_b_in['att_Wo'], 'L0_attn_b_cm_k': _L0_attn_b_in['cm_k'], 'L0_attn_b_cm_r': _L0_attn_b_in['cm_r'], 'L0_attn_b_ffn_Wk': _L0_attn_b_in['ffn_Wk'], 'L0_attn_b_ffn_Wr': _L0_attn_b_in['ffn_Wr'], 'L0_attn_b_ffn_Wv': _L0_attn_b_in['ffn_Wv'], 'L0_ffn_router_w': _L0_ffn_in['router_w'], 'L0_ffn_router_b': _L0_ffn_in['router_b'], 'L0_ffn_w1': _L0_ffn_in['w1'], 'L0_ffn_b1': _L0_ffn_in['b1'], 'L0_ffn_w2': _L0_ffn_in['w2'], 'L0_ffn_b2': _L0_ffn_in['b2'], 'L0_ffn_gamma': _L0_ffn_in['gamma'], 'L0_ffn_beta': _L0_ffn_in['beta']}
    _x0 = _d['L0_attn_a_hidden_states']
    _d['L0_attn_a_hidden_states'] = jax.random.normal(jax.random.fold_in(jax.random.key(seed), 1), (8, 512, 128), dtype=_x0.dtype)
    del _x0
    return _d

def reference(L0_attn_a_hidden_states, L0_attn_a_W_q, L0_attn_b_ln1_g, L0_attn_b_ln1_b, L0_attn_b_ln2_g, L0_attn_b_ln2_b, L0_attn_b_time_decay, L0_attn_b_time_first, L0_attn_b_time_mix_k, L0_attn_b_time_mix_v, L0_attn_b_time_mix_r, L0_attn_b_att_Wk, L0_attn_b_att_Wv, L0_attn_b_att_Wr, L0_attn_b_att_Wo, L0_attn_b_cm_k, L0_attn_b_cm_r, L0_attn_b_ffn_Wk, L0_attn_b_ffn_Wr, L0_attn_b_ffn_Wv, L0_ffn_router_w, L0_ffn_router_b, L0_ffn_w1, L0_ffn_b1, L0_ffn_w2, L0_ffn_b2, L0_ffn_gamma, L0_ffn_beta):

    def _L0_attn_a_ref(hidden_states, W_q):
        import jax, jax.numpy as jnp
        import numpy as np
        import math
        HIDDEN = 128
        NUM_LAYERS = 24
        INIT_RANGE = 0.02
        q = jnp.einsum('bsh,oh->bso', hidden_states, W_q)
        pre_attn = jnp.einsum('bso,bto->bst', q, hidden_states)
        attention = jnp.einsum('bst,bth->bsh', pre_attn, hidden_states)
        return attention

    def _L0_attn_b_ref(x, ln1_g, ln1_b, ln2_g, ln2_b, time_decay, time_first, time_mix_k, time_mix_v, time_mix_r, att_Wk, att_Wv, att_Wr, att_Wo, cm_k, cm_r, ffn_Wk, ffn_Wr, ffn_Wv):
        import jax, jax.numpy as jnp
        import numpy as np
        B, T, C = (8, 256, 128)
        NL, LID = (12, 1)
        H = 4 * C

        def _ln(x, g, b):
            m = x.mean(-1, keepdims=True)
            v = ((x - m) ** 2).mean(-1, keepdims=True)
            return (x - m) * jax.lax.rsqrt(v + 1e-05) * g + b

        def _shift(x):
            return jnp.pad(x, ((0, 0), (1, 0), (0, 0)))[:, :-1]

        def _wkv(time_decay, time_first, k, v):
            w = -jnp.exp(time_decay)
            kt = jnp.moveaxis(k, 1, 0)
            vt = jnp.moveaxis(v, 1, 0)
            Bb, Cc = (k.shape[0], k.shape[2])
            init = (jnp.zeros((Bb, Cc), k.dtype), jnp.zeros((Bb, Cc), k.dtype), jnp.full((Bb, Cc), -1e+38, k.dtype))

            def step(carry, kv_t):
                aa, bb, pp = carry
                kk, vv = kv_t
                ww = time_first + kk
                p = jnp.maximum(pp, ww)
                e1 = jnp.exp(pp - p)
                e2 = jnp.exp(ww - p)
                out = (e1 * aa + e2 * vv) / (e1 * bb + e2)
                ww2 = pp + w
                p2 = jnp.maximum(ww2, kk)
                e1b = jnp.exp(ww2 - p2)
                e2b = jnp.exp(kk - p2)
                return ((e1b * aa + e2b * vv, e1b * bb + e2b, p2), out)
            _, out = jax.lax.scan(step, init, (kt, vt))
            return jnp.moveaxis(out, 0, 1)
        xa = _ln(x, ln1_g, ln1_b)
        xx = _shift(xa)
        xk = xa * time_mix_k + xx * (1 - time_mix_k)
        xv = xa * time_mix_v + xx * (1 - time_mix_v)
        xr = xa * time_mix_r + xx * (1 - time_mix_r)
        k = jnp.einsum('btc,oc->bto', xk, att_Wk)
        v = jnp.einsum('btc,oc->bto', xv, att_Wv)
        r = jnp.einsum('btc,oc->bto', xr, att_Wr)
        rwkv = jax.nn.sigmoid(r) * _wkv(time_decay, time_first, k, v)
        x = x + jnp.einsum('bto,co->btc', rwkv, att_Wo)
        xc = _ln(x, ln2_g, ln2_b)
        xx2 = _shift(xc)
        xk2 = xc * cm_k + xx2 * (1 - cm_k)
        xr2 = xc * cm_r + xx2 * (1 - cm_r)
        kk = jnp.square(jax.nn.relu(jnp.einsum('btc,hc->bth', xk2, ffn_Wk)))
        kv = jnp.einsum('bth,ch->btc', kk, ffn_Wv)
        rkv = jax.nn.sigmoid(jnp.einsum('btc,oc->bto', xr2, ffn_Wr)) * kv
        return x + rkv

    def _L0_ffn_ref(tgt, router_w, router_b, w1, b1, w2, b2, gamma, beta):
        import jax, jax.numpy as jnp
        import numpy as np
        B, S, D, F, E = (2, 256, 128, 512, 8)
        LN_EPS = 1e-05

        def _xavier(key, shape, fan_in, fan_out):
            a = np.sqrt(6.0 / (fan_in + fan_out))
            return jax.random.uniform(key, shape, jnp.float32, -a, a)
        logits = jnp.einsum('bsd,ed->bse', tgt, router_w) + router_b
        rw = jax.nn.softmax(logits, axis=-1)
        rw = jnp.zeros_like(rw).at[..., 0].set(1.0)
        h = jax.nn.relu(jnp.einsum('bsd,edf->besf', tgt, w1) + b1[None, :, None, :])
        eo = jnp.einsum('besf,efd->besd', h, w2) + b2[None, :, None, :]
        tgt2 = jnp.einsum('besd,bse->bsd', eo, rw)
        x = tgt + tgt2
        mean = jnp.mean(x, axis=-1, keepdims=True)
        var = jnp.mean(jnp.square(x - mean), axis=-1, keepdims=True)
        return (x - mean) * jax.lax.rsqrt(var + LN_EPS) * gamma + beta
    x = L0_attn_a_hidden_states
    x = x + _L0_attn_a_ref(_layernorm(x, axis=-1), L0_attn_a_W_q)
    x = x + _L0_ffn_ref(_layernorm(x, axis=-1), L0_ffn_router_w, L0_ffn_router_b, L0_ffn_w1, L0_ffn_b1, L0_ffn_w2, L0_ffn_b2, L0_ffn_gamma, L0_ffn_beta)
    x = x + _L0_attn_b_ref(_layernorm(x, axis=-1), L0_attn_b_ln1_g, L0_attn_b_ln1_b, L0_attn_b_ln2_g, L0_attn_b_ln2_b, L0_attn_b_time_decay, L0_attn_b_time_first, L0_attn_b_time_mix_k, L0_attn_b_time_mix_v, L0_attn_b_time_mix_r, L0_attn_b_att_Wk, L0_attn_b_att_Wv, L0_attn_b_att_Wr, L0_attn_b_att_Wo, L0_attn_b_cm_k, L0_attn_b_cm_r, L0_attn_b_ffn_Wk, L0_attn_b_ffn_Wr, L0_attn_b_ffn_Wv)
    x = x + _L0_ffn_ref(_layernorm(x, axis=-1), L0_ffn_router_w, L0_ffn_router_b, L0_ffn_w1, L0_ffn_b1, L0_ffn_w2, L0_ffn_b2, L0_ffn_gamma, L0_ffn_beta)
    return x

_drawn_inputs = setup_inputs


def setup_inputs(seed=0):
    import zlib

    import numpy as np

    out = dict(_drawn_inputs(seed))
    spreads = {'L0_attn_b_ln1_g': (1.0, 0.6),
     'L0_attn_b_ln1_b': (0.0, 0.8),
     'L0_attn_b_ln2_g': (1.0, 0.6),
     'L0_attn_b_ln2_b': (0.0, 0.8),
     'L0_ffn_router_b': (0.0, 0.1),
     'L0_ffn_b1': (0.0, 0.1),
     'L0_ffn_b2': (0.0, 0.1),
     'L0_ffn_gamma': (1.0, 0.2),
     'L0_ffn_beta': (0.0, 0.1)}
    factors = {'L0_attn_b_time_decay': 8.0,
     'L0_attn_b_time_first': 8.0,
     'L0_attn_b_time_mix_k': 8.0,
     'L0_attn_b_time_mix_v': 8.0,
     'L0_attn_b_time_mix_r': 8.0,
     'L0_attn_b_att_Wk': 8.0,
     'L0_attn_b_att_Wv': 8.0,
     'L0_attn_b_att_Wr': 8.0,
     'L0_attn_b_att_Wo': 8.0,
     'L0_attn_b_cm_k': 8.0,
     'L0_attn_b_cm_r': 8.0,
     'L0_attn_b_ffn_Wk': 8.0,
     'L0_attn_b_ffn_Wr': 8.0,
     'L0_attn_b_ffn_Wv': 8.0}
    for name, (base, spread) in spreads.items():
        noise = np.random.default_rng([zlib.crc32(name.encode()), seed]).standard_normal(out[name].shape)
        drawn = base * np.exp(spread * noise) if base else spread * noise
        out[name] = jnp.asarray(drawn.astype(out[name].dtype))
    for name, factor in factors.items():
        out[name] = (out[name] * factor).astype(out[name].dtype)
    return out
```

```python
from contextlib import ExitStack

import concourse.bass as bass
from concourse import mybir
from concourse.alu_op_type import AluOpType as ALU

F32 = mybir.dt.float32
ACT = mybir.ActivationFunctionType

P = 128
EPS = 1e-5
MIN_LOG = -1e38
STAGES = 4
DMA = 16

VECTORS = ["ln1_g", "ln1_b", "ln2_g", "ln2_b", "decay", "first", "mix_k", "mix_v", "mix_r", "cm_k", "cm_r", "b2"]


class At:

    def __init__(self, values, offset):
        self.values, self.offset = values, offset
        self.done, self.before = values[1][offset + 1], values[1][offset]
        self.later = not isinstance(self.before, int) or self.before > 0

    def count(self, more=0, each=1):
        return self.values[each][self.offset + more]

    def turn(self, more):
        n = self.count(more)
        return n if not isinstance(n, int) or n > 0 else None


def hybrid_layer(nc, hidden, w_q, w1, w2, b1, wk, wv, wr, wo, f_wk, f_wr, f_wv, vectors, gamma, beta, out):
    B, T, C = hidden.shape
    J = T // P
    H = w1.shape[1] // P
    assert C == P and f_wk.shape[1] == H * P

    with ExitStack() as ctx:
        def sb(name, shape):
            return ctx.enter_context(nc.sbuf_tensor(name, shape, F32))

        def sem(name):
            return ctx.enter_context(nc.semaphore(name))

        def rows(name):
            return sb(name, [P, J, P])

        def cols(name):
            return sb(name, [P, T])

        Wq = sb("Wq", [P, C])
        W1 = sb("W1", [P, H * P])
        W2 = sb("W2", [P, H, C])
        Wk, Wv, Wr, Wo, FWr = (sb(n, [P, C]) for n in ("Wk", "Wv", "Wr", "Wo", "FWr"))
        FWk = sb("FWk", [P, H * P])
        FWv = sb("FWv", [P, H, C])
        B1 = sb("B1", [P, H])
        VEC = sb("VEC", [P, len(VECTORS)])
        GAMMA = sb("GAMMA", [P, C])
        BETA = sb("BETA", [P, J, C])
        IDENT = sb("IDENT", [P, P])
        ONE = sb("ONE", [P, 1])
        WDEC = sb("WDEC", [P, 1])
        WEXP = sb("WEXP", [P, 1])
        WROW = sb("WROW", [P, T])
        K_EPS, K_NEG, K_RSQRT = (sb(n, [P, 2 * J]) for n in ("K_EPS", "K_NEG", "K_RSQRT"))
        CARRY = sb("CARRY", [P, 1])

        def vec(name):
            n = VECTORS.index(name)
            return VEC[:, n:n + 1]

        bank_attn, bank_h, bank_z, bank_k, bank_v, bank_r, bank_c, bank_kv = (
            ctx.enter_context(nc.psum_tensor(n, [P, T], F32))
            for n in ("bank_attn", "bank_h", "bank_z", "bank_k", "bank_v", "bank_r", "bank_c", "bank_kv"))

        loaded = {n: sem("loaded_" + n) for n in ("first", "ffn", "tmix", "cmix")}
        const_ready = sem("const_ready")
        ident_ready = sem("ident_ready")
        decay_exp, decay_ready, decay_row = sem("decay_exp"), sem("decay_ready"), sem("decay_row")
        pads_ready = sem("pads_ready")

        class Norm:

            def __init__(self, n, kind="plain"):
                self.stats = sb(n + "_stats", [P, J, 6])
                self.mv = sb(n + "_mv", [P, J, 2])
                self.ve = sb(n + "_ve", [P, 2 * J])
                self.tmp = sb(n + "_tmp", [P, J])
                self.nm = sb(n + "_nm", [P, J])
                self.rs = sb(n + "_rs", [P, 2 * J])
                self.nb = sb(n + "_nb", [P, J])
                self.back = sb(n + "_back", [P, J])
                self.stats_done = sem(n + "_stats_done")
                self.mv_ready = sem(n + "_mv_ready")
                self.ve_ready = sem(n + "_ve_ready")
                self.rs_ready = sem(n + "_rs_ready")
                if kind != "scale only":
                    self.nb_ready = sem(n + "_nb_ready")
                if kind == "twice":
                    self.tmp_ready = sem(n + "_tmp_ready")
                    self.q_ready = sem(n + "_q_ready")

        class Ffn:

            def __init__(self, n, x, x_ready, y_out, out_used, out_each):
                self.x, self.x_ready = x, x_ready
                self.norm, self.znorm = Norm(n + "_y"), Norm(n + "_z", "scale only")
                self.xb, self.xb_ready = rows(n + "_xb"), sem(n + "_xb_ready")
                self.y, self.y_ready = rows(n + "_y"), sem(n + "_y_ready")
                self.yT_psum, self.yT_ready = sem(n + "_yT_psum"), sem(n + "_yT_ready")
                self.yT = cols(n + "_yT")
                self.yTb, self.yTb_ready = cols(n + "_yTb"), sem(n + "_yTb_ready")
                self.h = sb(n + "_h", [P, H, T])
                self.h_psum = [sem(f"{n}_h{f}_psum") for f in range(H)]
                self.h_ready = [sem(f"{n}_h{f}_ready") for f in range(H)]
                self.z_psum = sem(n + "_z_psum")
                self.zg, self.zg_ready = rows(n + "_zg"), sem(n + "_zg_ready")
                self.out, self.out_ready = y_out, sem(n + "_out_ready")
                self.out_used, self.out_each = out_used, out_each

        X0, x0_loaded = rows("X0"), sem("x0_loaded")
        na = Norm("attn")
        XN, xn_ready = rows("XN"), sem("xn_ready")
        xnT_psum, xnT_ready = sem("xnT_psum"), sem("xnT_ready")
        XNT = cols("XNT")
        GRAM, gram_psum, gram_ready = sb("GRAM", [P, C]), sem("gram_psum"), sem("gram_ready")
        PROJ, proj_psum, proj_ready = sb("PROJ", [P, C]), sem("proj_psum"), sem("proj_ready")
        attn_psum = sem("attn_psum")
        X1, x1_ready = rows("X1"), sem("x1_ready")
        X2, X3, X4 = rows("X2"), rows("X3"), rows("X4")

        x2_kept = sem("x2_kept")
        stored = sem("stored")
        nt = Norm("tmix", "twice")
        X2K = rows("X2K")
        back_half, back_ready = sem("back_half"), sem("back_ready")
        N, n_ready = rows("N"), sem("n_ready")
        nT_psum = sem("nT_psum")
        XA, xa_ready = sb("XA", [P, T + 1]), sem("xa_ready")
        DX, dx_ready = cols("DX"), sem("dx_ready")
        XK, xk_ready = cols("XK"), sem("xk_ready")
        XV, xv_ready = cols("XV"), sem("xv_ready")
        XR, xr_ready = cols("XR"), sem("xr_ready")
        k_psum, v_psum, r_psum = sem("k_psum"), sem("v_psum"), sem("r_psum")
        PP, pp_ready = sb("PP", [P, T + 1]), sem("pp_ready")
        DIFF, diff_ready = sb("DIFF", [P, 2, T]), sem("diff_ready")
        LOW, low_ready = sb("LOW", [P, 2, T]), sem("low_ready")
        HIGH, high_ready = sb("HIGH", [P, 2, T]), sem("high_ready")
        EA, ea_ready = sb("EA", [P, 3, T]), sem("ea_ready")
        EB, eb_ready = sb("EB", [P, 2, T]), sem("eb_ready")
        EV, ev_ready = cols("EV"), sem("ev_ready")
        AB, ab_ready = sb("AB", [P, 2, T + 1]), sem("ab_ready")
        m2_ready = sem("m2_ready")
        M1, m1_ready = sb("M1", [P, 2, T]), sem("m1_ready")
        ND, nd_ready = sb("ND", [P, 2, T]), sem("nd_ready")
        AR, ar_ready = cols("AR"), sem("ar_ready")
        ER, er_ready = cols("ER"), sem("er_ready")
        DN, dn_ready = cols("DN"), sem("dn_ready")
        LD, ld_ready = cols("LD"), sem("ld_ready")
        RL, rl_ready = cols("RL"), sem("rl_ready")
        RC, rc_ready = cols("RC"), sem("rc_ready")
        RW, rw_ready = cols("RW"), sem("rw_ready")
        o_psum = sem("o_psum")
        U1, u1_ready = rows("U1"), sem("u1_ready")
        X2U, x2u_ready = rows("X2U"), sem("x2u_ready")

        ncm = Norm("cmix")
        NC, nc_ready = rows("NC"), sem("nc_ready")
        ncT_psum = sem("ncT_psum")
        XC, xc_ready = sb("XC", [P, T + 1]), sem("xc_ready")
        DC, dc_ready = cols("DC"), sem("dc_ready")
        XK2, xk2_ready = cols("XK2"), sem("xk2_ready")
        XR2, xr2_ready = cols("XR2"), sem("xr2_ready")
        kk_psum = [sem(f"kk{f}_psum") for f in range(H)]
        KR, kr_ready = sb("KR", [P, H, T]), [sem(f"kr{f}_ready") for f in range(H)]
        KK, kk_ready = sb("KK", [P, H, T]), [sem(f"kk{f}_ready") for f in range(H)]
        kv_psum, r2_psum = sem("kv_psum"), sem("r2_psum")
        AR2, ar2_ready = cols("AR2"), sem("ar2_ready")
        ER2, er2_ready = cols("ER2"), sem("er2_ready")
        LD2, ld2_ready = cols("LD2"), sem("ld2_ready")
        RL2, rl2_ready = cols("RL2"), sem("rl2_ready")
        SG, sg_ready = cols("SG"), sem("sg_ready")
        KVS, kvs_ready = cols("KVS"), sem("kvs_ready")
        x3_ready = sem("x3_ready")

        f1 = Ffn("f1", X1, x1_ready, X2, [(x2_kept, DMA), (n_ready, 1)], 1)
        f2 = Ffn("f2", X3, x3_ready, X4, [(stored, DMA)], 16)
        x2_ready, x4_ready = f1.out_ready, f2.out_ready

        def each_iteration(engines, body, after_first=None, dma_counts=()):
            first, last = STAGES, B
            stages = lambda values, i: [
                At(values, -s) if i is None or 0 <= i - s < B else None for s in range(STAGES)]
            span = range(-STAGES - 4, STAGES + 2)

            def numbers(i):
                return {each: {k: min(i + k, B) * each for k in span} for each in (1, DMA)}

            for i in range(first):
                body(*stages(numbers(i), i))
                if i == 0 and after_first is not None:
                    after_first()
            with engines.Fori(first, last) as i:
                def held(value, name):
                    register = engines.alloc_register(name)
                    engines.reg_mov(register, value)
                    return engines.snap(register)

                registers = {1: {k: held(i + k, f"n{k + STAGES}") for k in range(-STAGES + 1, 2)}}
                registers[DMA] = {k: held((i + k) * DMA, f"dma{k + STAGES}") for k in dma_counts}
                body(*stages(registers, None))
            for i in range(last, B + STAGES - 1):
                body(*stages(numbers(i), i))

        block = ctx.enter_context(nc.Block())

        @block.sync
        def _(sp):
            x0_dram = hidden.rearrange("b t c -> (b t) c")
            out_dram = out.rearrange("b t c -> (b t) c")

            def load_x0(b):
                if b.later:
                    sp.wait_ge(x1_ready, b.before)
                sp.dma_start(X0[:], of(x0_dram, b)).then_inc(x0_loaded, DMA)

            def keep_x2(b):
                sp.wait_ge(x2_ready, b.done)
                if b.later:
                    sp.wait_ge(x2u_ready, b.before)
                sp.dma_start(X2K[:], X2[:]).then_inc(x2_kept, DMA)

            def store(b):
                sp.wait_ge(x4_ready, b.done)
                sp.dma_start(of(out_dram, b), X4[:]).then_inc(stored, DMA)

            def of(dram, b):
                return dram[bass.ds(b.count() * T, T), :].rearrange("(j p) c -> p j c", p=P)

            def iteration(h, t, c, g):
                if h is not None:
                    load_x0(h)
                if t is not None:
                    keep_x2(t)
                if g is not None:
                    store(g)

            def weights():
                sp.dma_start(Wq[:], w_q).then_inc(loaded["first"], 16)
                sp.dma_start(VEC[:], vectors).then_inc(loaded["first"], 16)
                sp.dma_start(W1[:], w1).then_inc(loaded["ffn"], 16)
                sp.dma_start(B1[:], b1).then_inc(loaded["ffn"], 16)
                sp.dma_start(W2[:], w2.rearrange("(f p) c -> p f c", p=P)).then_inc(loaded["ffn"], 16)
                sp.dma_start(GAMMA[:], gamma).then_inc(loaded["ffn"], 16)
                sp.dma_start(BETA[:].rearrange("p j c -> p (j c)"), beta).then_inc(loaded["ffn"], 16)
                for t, d in ((Wk, wk), (Wv, wv), (Wr, wr), (Wo, wo)):
                    sp.dma_start(t[:], d).then_inc(loaded["tmix"], 16)
                sp.dma_start(FWk[:], f_wk).then_inc(loaded["cmix"], 16)
                sp.dma_start(FWr[:], f_wr).then_inc(loaded["cmix"], 16)
                sp.dma_start(FWv[:], f_wv.rearrange("(f p) c -> p f c", p=P)).then_inc(loaded["cmix"], 16)

            each_iteration(sp, iteration, after_first=weights)
            sp.wait_ge(stored, DMA * B)

        @block.gpsimd
        def _(pool):
            pool.memset(K_EPS[:], EPS).then_inc(const_ready, 1)
            pool.memset(K_NEG[:], -1.0).then_inc(const_ready, 1)
            pool.memset(K_RSQRT[:], -0.5).then_inc(const_ready, 1)
            pool.memset(ONE[:], 1.0).then_inc(const_ready, 1)
            pool.memset(IDENT[:], 0.0).then_inc(const_ready, 1)
            pool.wait_ge(const_ready, 5)
            pool.affine_select(out=IDENT[:], in_=IDENT[:], compare_op=ALU.not_equal, fill=1.0, base=0,
                               pattern=[[-1, P]], channel_multiplier=1).then_inc(ident_ready, 1)
            pool.memset(XA[:, 0:1], 0.0).then_inc(pads_ready, 1)
            pool.memset(XC[:, 0:1], 0.0).then_inc(pads_ready, 1)
            pool.memset(AB[:, :, 0:1], 0.0).then_inc(pads_ready, 1)
            pool.memset(PP[:, 0:1], MIN_LOG).then_inc(pads_ready, 1)

            def scale(b, n, users, with_bias=True):
                pool.wait_ge(n.mv_ready, b.done)
                for s in users:
                    if b.later:
                        pool.wait_ge(s, b.before)
                if with_bias:
                    pool.tensor_tensor(n.nm[:], n.mv[:, :, 0], K_NEG[:, 0:J], ALU.mult)
                pool.tensor_tensor(n.ve[:, 0:J], n.mv[:, :, 1], K_EPS[:, 0:J], ALU.add).then_inc(n.ve_ready, 1)
                pool.wait_ge(n.ve_ready, b.done)
                pool.tensor_tensor(n.rs[:, 0:J], n.ve[:, 0:J], K_RSQRT[:, 0:J], ALU.pow).then_inc(n.rs_ready, 1)
                if with_bias:
                    pool.wait_ge(n.rs_ready, b.done)
                    pool.tensor_tensor(n.nb[:], n.nm[:], n.rs[:, 0:J], ALU.mult).then_inc(n.nb_ready, 1)

            def scale_twice(b, n):
                pool.wait_ge(n.mv_ready, b.done)
                if b.later:
                    pool.wait_ge(u1_ready, b.before)
                if b.later:
                    pool.wait_ge(n_ready, b.before)
                pool.tensor_tensor(n.nm[:], n.mv[:, :, 0], K_NEG[:, 0:J], ALU.mult)
                pool.tensor_tensor(n.ve[:, J:], n.mv[:, :, 1], K_EPS[:, 0:J], ALU.add).then_inc(n.ve_ready, 1)
                pool.wait_ge(n.ve_ready, b.done)
                pool.tensor_tensor(n.tmp[:], n.ve[:, J:], K_EPS[:, 0:J], ALU.mult).then_inc(n.tmp_ready, 1)
                pool.wait_ge(n.tmp_ready, b.done)
                pool.tensor_tensor(n.ve[:, 0:J], n.mv[:, :, 1], n.tmp[:], ALU.add).then_inc(n.q_ready, 1)
                pool.wait_ge(n.q_ready, b.done)
                pool.tensor_tensor(n.rs[:], n.ve[:], K_RSQRT[:], ALU.pow).then_inc(n.rs_ready, 1)
                pool.wait_ge(n.rs_ready, b.done)
                pool.tensor_tensor(n.nb[:], n.nm[:], n.rs[:, 0:J], ALU.mult).then_inc(n.nb_ready, 1)
                pool.tensor_tensor(n.tmp[:], n.ve[:, 0:J], n.rs[:, 0:J], ALU.mult).then_inc(back_half, 1)
                pool.wait_ge(back_half, b.done)
                pool.tensor_tensor(n.back[:], n.tmp[:], n.rs[:, J:], ALU.mult).then_inc(back_ready, 1)

            def iteration(h, t, c, g):
                if g is not None:
                    scale(g, f2.norm, [f2.y_ready])
                if c is not None:
                    scale(c, ncm, [nc_ready])
                if t is not None:
                    scale_twice(t, nt)
                if h is not None:
                    scale(h, na, [xn_ready])
                if g is not None:
                    scale(g, f2.znorm, [f2.out_ready], with_bias=False)
                if h is not None:
                    scale(h, f1.norm, [f1.y_ready])
                    scale(h, f1.znorm, [f1.out_ready], with_bias=False)

            each_iteration(pool, iteration)

        @block.vector
        def _(dve):
            v = nc.vector

            def stats(b, n, src, src_ready, each=1):
                dve.wait_ge(src_ready, b.count(1, each))
                if b.later:
                    dve.wait_ge(n.mv_ready, b.before)
                for j in range(J):
                    last = v.bn_stats(n.stats[:, j, :], src[:, j, :])
                last.then_inc(n.stats_done, 1)

            def mean_var(b, n, scale_ready):
                if b.later:
                    dve.wait_ge(scale_ready, b.before)
                dve.wait_ge(n.stats_done, b.done)
                v.memset(CARRY[:], 0.0)
                for j in range(J):
                    last = v.bn_aggr(n.mv[:, j, :], n.stats[:, j, :])
                last.then_inc(n.mv_ready, 1)

            def attn_out(b):
                dve.wait_ge(attn_psum, b.done)
                if b.later:
                    dve.wait_ge(f1.y_ready, b.before)
                if b.later:
                    dve.wait_ge(f1.xb_ready, b.before)
                v.tensor_tensor(X1[:], bank_attn[:].rearrange("p (j c) -> p j c", j=J), X0[:], ALU.add).then_inc(x1_ready, 1)

            def ffn_residual(b, f):
                dve.wait_ge(f.x_ready, b.done)
                if b.later:
                    dve.wait_ge(f.out_ready, b.before)
                v.tensor_tensor(f.xb[:], f.x[:], BETA[:], ALU.add).then_inc(f.xb_ready, 1)

            def ffn_y_bias(b, f):
                dve.wait_ge(f.yT_ready, b.done)
                if b.later:
                    dve.wait_ge(f.z_psum, b.before)
                v.tensor_scalar(f.yTb[:], f.yT[:], vec("b2"), None, ALU.add).then_inc(f.yTb_ready, 1)

            bank_z_rows = bank_z[:].rearrange("p (j c) -> p j c", j=J)

            def ffn_gain(b, f):
                dve.wait_ge(f.znorm.mv_ready, b.done)
                if b.later:
                    dve.wait_ge(f.out_ready, b.before)
                for j in range(J):
                    last = v.scalar_tensor_tensor(f.zg[:, j, :], bank_z_rows[:, j, :], f.znorm.mv[:, j, 0:1], GAMMA[:],
                                                  ALU.subtract, ALU.mult)
                last.then_inc(f.zg_ready, 1)

            def ffn_out(b, f):
                dve.wait_ge(f.znorm.rs_ready, b.done)
                dve.wait_ge(f.zg_ready, b.done)
                dve.wait_ge(f.xb_ready, b.done)
                for s, each in f.out_used:
                    if b.later:
                        dve.wait_ge(s, b.count(0, each))
                for j in range(J):
                    last = v.scalar_tensor_tensor(f.out[:, j, :], f.zg[:, j, :], f.znorm.rs[:, j:j + 1], f.xb[:, j, :],
                                                  ALU.mult, ALU.add)
                last.then_inc(f.out_ready, 1)

            def mix(b, x, x_ready, diff, diff_ready, mixes):
                dve.wait_ge(x_ready, b.done)
                if b.later:
                    dve.wait_ge(mixes[-1][2], b.before)
                v.tensor_tensor(diff[:], x[:, 1:], x[:, 0:T], ALU.subtract).then_inc(diff_ready, 1)
                dve.wait_ge(diff_ready, b.done)
                for m, dst, dst_ready, dst_used in mixes:
                    if b.later:
                        dve.wait_ge(dst_used, b.before)
                    v.scalar_tensor_tensor(dst[:], diff[:], vec(m), x[:, 0:T], ALU.mult, ALU.add).then_inc(dst_ready, 1)

            def running_max(b):
                dve.wait_ge(k_psum, b.done)
                if b.later:
                    dve.wait_ge(diff_ready, b.before)
                v.tensor_tensor_scan(PP[:, 1:], WROW[:], bank_k[:], MIN_LOG, ALU.add, ALU.max).then_inc(pp_ready, 1)

            def differences(b):
                dve.wait_ge(pp_ready, b.done)
                if b.later:
                    dve.wait_ge(low_ready, b.before)
                if b.later:
                    dve.wait_ge(high_ready, b.before)
                v.scalar_tensor_tensor(DIFF[:, 0, :], PP[:, 0:T], WDEC[:], bank_k[:], ALU.add, ALU.subtract)
                v.scalar_tensor_tensor(DIFF[:, 1, :], bank_k[:], vec("first"), PP[:, 0:T],
                                       ALU.add, ALU.subtract).then_inc(diff_ready, 1)

            def exponents(b):
                dve.wait_ge(diff_ready, b.done)
                if b.later:
                    dve.wait_ge(ea_ready, b.before)
                v.tensor_scalar(LOW[:], DIFF[:], 0.0, None, ALU.min).then_inc(low_ready, 1)
                if b.later:
                    dve.wait_ge(eb_ready, b.before)
                v.tensor_scalar(HIGH[:], DIFF[:], 0.0, None, ALU.max).then_inc(high_ready, 1)

            def sums(b):
                dve.wait_ge(eb_ready, b.done)
                dve.wait_ge(v_psum, b.done)
                if b.later:
                    dve.wait_ge(ab_ready, b.before)
                v.tensor_tensor(EV[:], EB[:, 0, :], bank_v[:], ALU.mult).then_inc(ev_ready, 1)
                dve.wait_ge(ea_ready, b.done)
                if b.later:
                    dve.wait_ge(m1_ready, b.before)
                v.tensor_tensor_scan(AB[:, 1, 1:], EA[:, 0, :], EB[:, 0, :], 0.0, ALU.mult, ALU.add)
                if b.later:
                    dve.wait_ge(nd_ready, b.before)
                v.tensor_tensor(EA[:, 1, :], EA[:, 2, :], bank_v[:], ALU.mult).then_inc(m2_ready, 1)
                dve.wait_ge(ev_ready, b.done)
                v.tensor_tensor_scan(AB[:, 0, 1:], EA[:, 0, :], EV[:], 0.0, ALU.mult, ALU.add).then_inc(ab_ready, 1)

            def weighted(b):
                dve.wait_ge(ab_ready, b.done)
                if b.later:
                    dve.wait_ge(nd_ready, b.before)
                v.tensor_tensor(M1[:], AB[:, :, 0:T], EB[:, 1:2, :].broadcast_to([P, 2, T]), ALU.mult).then_inc(m1_ready, 1)
                dve.wait_ge(m1_ready, b.done)
                dve.wait_ge(m2_ready, b.done)
                if b.later:
                    dve.wait_ge(rw_ready, b.before)
                if b.later:
                    dve.wait_ge(dn_ready, b.before)
                v.tensor_tensor(ND[:], M1[:], EA[:, 1:3, :], ALU.add).then_inc(nd_ready, 1)

            def gate_sum(b):
                dve.wait_ge(nd_ready, b.done)
                dve.wait_ge(er_ready, b.done)
                if b.later:
                    dve.wait_ge(ld_ready, b.before)
                v.scalar_tensor_tensor(DN[:], ER[:], 1.0, ND[:, 1, :], ALU.add, ALU.mult).then_inc(dn_ready, 1)

            def gate_log(b):
                dve.wait_ge(ld_ready, b.done)
                if b.later:
                    dve.wait_ge(rc_ready, b.before)
                v.scalar_tensor_tensor(RL[:], bank_r[:], 0.0, LD[:], ALU.min, ALU.subtract).then_inc(rl_ready, 1)

            def gated(b):
                dve.wait_ge(rc_ready, b.done)
                if b.later:
                    dve.wait_ge(o_psum, b.before)
                v.tensor_tensor(RW[:], ND[:, 0, :], RC[:], ALU.mult).then_inc(rw_ready, 1)

            def tmix_out(b):
                dve.wait_ge(o_psum, b.done)
                dve.wait_ge(back_ready, b.done)
                if b.later:
                    dve.wait_ge(nc_ready, b.before)
                if b.later:
                    dve.wait_ge(x2u_ready, b.before)
                o = bank_k[:].rearrange("p (j c) -> p j c", j=J)
                for j in range(J):
                    last = v.scalar_tensor_tensor(U1[:, j, :], N[:, j, :], nt.back[:, j:j + 1], o[:, j, :],
                                                  ALU.mult, ALU.add)
                last.then_inc(u1_ready, 1)

            def tmix_residual(b):
                dve.wait_ge(u1_ready, b.done)
                dve.wait_ge(x2_kept, b.count(1, DMA))
                if b.later:
                    dve.wait_ge(x3_ready, b.before)
                v.tensor_tensor(X2U[:], X2K[:], U1[:], ALU.add).then_inc(x2u_ready, 1)

            def cgate_log(b):
                dve.wait_ge(ld2_ready, b.done)
                if b.later:
                    dve.wait_ge(sg_ready, b.before)
                v.scalar_tensor_tensor(RL2[:], bank_c[:], 0.0, LD2[:], ALU.min, ALU.subtract).then_inc(rl2_ready, 1)

            def cmix_out(b):
                dve.wait_ge(sg_ready, b.done)
                dve.wait_ge(kv_psum, b.done)
                if b.later:
                    dve.wait_ge(x3_ready, b.before)
                v.tensor_tensor(KVS[:], bank_kv[:], SG[:], ALU.mult).then_inc(kvs_ready, 1)
                dve.wait_ge(kvs_ready, b.done)
                dve.wait_ge(x2u_ready, b.done)
                if b.later:
                    dve.wait_ge(f2.y_ready, b.before)
                if b.later:
                    dve.wait_ge(f2.xb_ready, b.before)
                v.tensor_tensor(X3[:], KVS[:].rearrange("p (j c) -> p j c", j=J), X2U[:], ALU.add).then_inc(x3_ready, 1)

            time_mixes = [("mix_k", XK, xk_ready, k_psum), ("mix_v", XV, xv_ready, v_psum), ("mix_r", XR, xr_ready, r_psum)]
            channel_mixes = [("cm_k", XK2, xk2_ready, kk_psum[H - 1]), ("cm_r", XR2, xr2_ready, r2_psum)]

            def iteration(h, t, c, g):
                if g is not None:
                    stats(g, f2.norm, X3, x3_ready)
                    mean_var(g, f2.norm, f2.norm.nb_ready)
                if c is not None:
                    stats(c, ncm, U1, u1_ready)
                    mean_var(c, ncm, ncm.nb_ready)
                if t is not None:
                    stats(t, nt, X2, x2_ready)
                    mean_var(t, nt, back_ready)
                if h is not None:
                    stats(h, na, X0, x0_loaded, each=DMA)
                    mean_var(h, na, na.nb_ready)
                if g is not None:
                    ffn_residual(g, f2)
                    ffn_y_bias(g, f2)
                if c is not None:
                    mix(c, XC, xc_ready, DC, dc_ready, channel_mixes)
                if t is not None:
                    mix(t, XA, xa_ready, DX, dx_ready, time_mixes)
                    running_max(t)
                    differences(t)
                    exponents(t)
                if h is not None:
                    attn_out(h)
                    stats(h, f1.norm, X1, x1_ready)
                    mean_var(h, f1.norm, f1.norm.nb_ready)
                    ffn_residual(h, f1)
                if g is not None:
                    stats(g, f2.znorm, bank_z_rows, f2.z_psum)
                    mean_var(g, f2.znorm, f2.znorm.rs_ready)
                    ffn_gain(g, f2)
                    ffn_out(g, f2)
                if t is not None:
                    sums(t)
                    weighted(t)
                    gate_sum(t)
                if h is not None:
                    ffn_y_bias(h, f1)
                if t is not None:
                    gate_log(t)
                if c is not None:
                    cgate_log(c)
                if t is not None:
                    gated(t)
                if c is not None:
                    cmix_out(c)
                if t is not None:
                    tmix_out(t)
                    tmix_residual(t)
                if h is not None:
                    stats(h, f1.znorm, bank_z_rows, f1.z_psum)
                    mean_var(h, f1.znorm, f1.znorm.rs_ready)
                    ffn_gain(h, f1)
                    ffn_out(h, f1)

            dve.wait_ge(loaded["first"], 32)
            dve.wait_ge(decay_ready, 1)
            v.memset(WROW[:], 0.0).then_inc(decay_row, 1)
            dve.wait_ge(decay_row, 1)
            v.tensor_scalar(WROW[:], WROW[:], WDEC[:], None, ALU.add).then_inc(decay_row, 1)
            dve.wait_ge(decay_row, 2)
            dve.wait_ge(pads_ready, 4)
            dve.wait_ge(loaded["ffn"], 80)
            each_iteration(dve, iteration, dma_counts=(1, 0, 1 - STAGES))

        @block.scalar
        def _(act):
            a = nc.scalar

            def normed(b, n, src, dst, dst_ready, dst_used):
                act.wait_ge(n.nb_ready, b.done)
                for s in dst_used:
                    if b.later:
                        act.wait_ge(s, b.before)
                for j in range(J):
                    last = a.activation(dst[:, j, :], src[:, j, :], ACT.Identity, scale=n.rs[:, j:j + 1], bias=n.nb[:, j:j + 1])
                last.then_inc(dst_ready, 1)

            def evacuate(b, src, src_ready, dst, dst_ready, dst_used):
                act.wait_ge(src_ready, b.done)
                for s in dst_used:
                    if b.later:
                        act.wait_ge(s, b.before)
                a.activation(dst, src, ACT.Copy).then_inc(dst_ready, 1)

            def evacuate_affine(b, src_ready, bank, dst, gain, shift, dst_ready, dst_used):
                act.wait_ge(src_ready, b.done)
                if b.later:
                    act.wait_ge(dst_used, b.before)
                a.activation(dst[:, 1:], bank[:], ACT.Identity, scale=vec(gain), bias=vec(shift)).then_inc(dst_ready, 1)

            def ffn_hidden(b, f, n):
                act.wait_ge(f.h_psum[n], b.done)
                if b.later:
                    act.wait_ge(f.z_psum, b.before)
                a.activation(f.h[:, n, :], bank_h[:], ACT.Relu, bias=B1[:, n:n + 1]).then_inc(f.h_ready[n], 1)

            def exp_low(b):
                act.wait_ge(low_ready, b.done)
                if b.later:
                    act.wait_ge(nd_ready, b.before)
                a.activation(EA[:, 0:3:2, :], LOW[:], ACT.Exp).then_inc(ea_ready, 1)

            def exp_high(b):
                act.wait_ge(high_ready, b.done)
                if b.later:
                    act.wait_ge(m1_ready, b.before)
                a.activation(EB[:], HIGH[:], ACT.Exp, scale=-1.0).then_inc(eb_ready, 1)

            def one(b, dst, src, func, src_ready, dst_ready, dst_used, **more):
                act.wait_ge(src_ready, b.done)
                if b.later:
                    act.wait_ge(dst_used, b.before)
                a.activation(dst[:], src[:], func, **more).then_inc(dst_ready, 1)

            def squared_relu(b, n):
                act.wait_ge(kk_psum[n], b.done)
                if b.later:
                    act.wait_ge(kk_ready[n], b.before)
                a.activation(KR[:, n, :], bank_c[:], ACT.Relu).then_inc(kr_ready[n], 1)
                act.wait_ge(kr_ready[n], b.done)
                if b.later:
                    act.wait_ge(kv_psum, b.before)
                a.activation(KK[:, n, :], KR[:, n, :], ACT.Square).then_inc(kk_ready[n], 1)

            def iteration(h, t, c, g):
                if g is not None:
                    normed(g, f2.norm, X3, f2.y, f2.y_ready, [f2.yT_psum])
                if c is not None:
                    normed(c, ncm, U1, NC, nc_ready, [ncT_psum])
                if t is not None:
                    normed(t, nt, X2, N, n_ready, [nT_psum, u1_ready])
                if g is not None:
                    evacuate(g, bank_h[:], f2.yT_psum, f2.yT[:], f2.yT_ready, [f2.h_psum[H - 1], f2.yTb_ready])
                if c is not None:
                    evacuate_affine(c, ncT_psum, bank_c, XC, "ln2_g", "ln2_b", xc_ready, xr2_ready)
                if t is not None:
                    evacuate_affine(t, nT_psum, bank_k, XA, "ln1_g", "ln1_b", xa_ready, xr_ready)
                if h is not None:
                    normed(h, na, X0, XN, xn_ready, [gram_psum])
                    evacuate(h, bank_attn[:], xnT_psum, XNT[:], xnT_ready, [attn_psum])
                if g is not None:
                    ffn_hidden(g, f2, 0)
                    ffn_hidden(g, f2, 1)
                if h is not None:
                    evacuate(h, bank_attn[:, 0:C], gram_psum, GRAM[:], gram_ready, [proj_psum])
                    evacuate(h, bank_attn[:, C:2 * C], proj_psum, PROJ[:], proj_ready, [attn_psum])
                if g is not None:
                    ffn_hidden(g, f2, 2)
                    ffn_hidden(g, f2, 3)
                if t is not None:
                    exp_high(t)
                    exp_low(t)
                    one(t, AR, bank_r, ACT.Abs, r_psum, ar_ready, er_ready)
                    one(t, ER, AR, ACT.Exp, ar_ready, er_ready, dn_ready, scale=-1.0)
                if h is not None:
                    normed(h, f1.norm, X1, f1.y, f1.y_ready, [f1.yT_psum])
                    evacuate(h, bank_h[:], f1.yT_psum, f1.yT[:], f1.yT_ready, [f1.h_psum[H - 1], f1.yTb_ready])
                if c is not None:
                    for n in range(H):
                        squared_relu(c, n)
                if t is not None:
                    one(t, LD, DN, ACT.Ln, dn_ready, ld_ready, rl_ready)
                if c is not None:
                    one(c, AR2, bank_c, ACT.Abs, r2_psum, ar2_ready, er2_ready)
                    one(c, ER2, AR2, ACT.Exp, ar2_ready, er2_ready, ld2_ready, scale=-1.0)
                    one(c, LD2, ER2, ACT.Ln, er2_ready, ld2_ready, rl2_ready, bias=ONE[:])
                if t is not None:
                    one(t, RC, RL, ACT.Exp, rl_ready, rc_ready, rw_ready)
                if c is not None:
                    one(c, SG, RL2, ACT.Exp, rl2_ready, sg_ready, kvs_ready)
                if h is not None:
                    for n in range(H):
                        ffn_hidden(h, f1, n)

            a.preload_act_table_set("natural_log_exp_and_others")
            act.wait_ge(loaded["first"], 32)
            a.activation(WEXP[:], vec("decay"), ACT.Exp).then_inc(decay_exp, 1)
            act.wait_ge(decay_exp, 1)
            a.mul(WDEC[:], WEXP[:], -1.0).then_inc(decay_ready, 1)
            act.wait_ge(const_ready, 5)
            act.wait_ge(pads_ready, 4)
            act.wait_ge(loaded["ffn"], 80)
            each_iteration(act, iteration)

        @block.tensor
        def _(pe):
            t_ = nc.tensor

            def transposed(b, src, bank, done):
                for j in range(J):
                    last = t_.transpose(bank[:, j * P:(j + 1) * P], src[:, j, :], IDENT[:])
                last.then_inc(done, 1)

            def attn_transpose(b):
                pe.wait_ge(xn_ready, b.done)
                if b.later:
                    pe.wait_ge(x1_ready, b.before)
                transposed(b, XN, bank_attn, xnT_psum)

            def attn_gram(b):
                pe.wait_ge(xnT_ready, b.done)
                for j in range(J):
                    last = t_.matmul(bank_attn[:, 0:C], XN[:, j, :], XN[:, j, :], start=(j == 0), stop=(j == J - 1))
                last.then_inc(gram_psum, 1)

            def attn_proj(b):
                pe.wait_ge(gram_ready, b.done)
                t_.matmul(bank_attn[:, C:2 * C], Wq[:], GRAM[:], start=True, stop=True).then_inc(proj_psum, 1)

            def attn_apply(b):
                pe.wait_ge(proj_ready, b.done)
                for j in range(J):
                    last = t_.matmul(bank_attn[:, j * C:(j + 1) * C], XNT[:, j * P:(j + 1) * P], PROJ[:], start=True, stop=True)
                last.then_inc(attn_psum, 1)

            def ffn_transpose(b, f, other, turn):
                pe.wait_ge(f.y_ready, b.done)
                if turn is not None:
                    pe.wait_ge(other.h_ready[H - 1], turn)
                transposed(b, f.y, bank_h, f.yT_psum)

            def ffn_hidden(b, f, n):
                pe.wait_ge(f.yT_ready if n == 0 else f.h_ready[n - 1], b.done)
                t_.matmul(bank_h[:], W1[:, n * P:(n + 1) * P], f.yT[:], start=True, stop=True).then_inc(f.h_psum[n], 1)

            def ffn_start(b, f, other, turn):
                pe.wait_ge(f.yTb_ready, b.done)
                if turn is not None:
                    pe.wait_ge(other.zg_ready, turn)
                for j in range(J):
                    t_.matmul(bank_z[:, j * C:(j + 1) * C], f.yTb[:, j * P:(j + 1) * P], IDENT[:], start=(j == 0), stop=False,
                              skip_group_check=True)

            def ffn_down(b, f, n):
                pe.wait_ge(f.h_ready[n], b.done)
                for j in range(J):
                    last = t_.matmul(bank_z[:, j * C:(j + 1) * C], f.h[:, n, j * P:(j + 1) * P], W2[:, n, :], start=False,
                                     stop=(n == H - 1), skip_group_check=True)
                if n == H - 1:
                    last.then_inc(f.z_psum, 1)

            def tmix_transpose(b):
                pe.wait_ge(n_ready, b.done)
                if b.later:
                    pe.wait_ge(u1_ready, b.before)
                transposed(b, N, bank_k, nT_psum)

            def tmix_product(b, x, x_ready, w, bank, done, bank_used):
                pe.wait_ge(x_ready, b.done)
                if bank_used is not None:
                    if b.later:
                        pe.wait_ge(bank_used, b.before)
                t_.matmul(bank[:], w[:], x[:], start=True, stop=True).then_inc(done, 1)

            def tmix_o(b):
                pe.wait_ge(rw_ready, b.done)
                for j in range(J):
                    last = t_.matmul(bank_k[:, j * C:(j + 1) * C], RW[:, j * P:(j + 1) * P], Wo[:], start=True, stop=True)
                last.then_inc(o_psum, 1)

            def cmix_transpose(b):
                pe.wait_ge(nc_ready, b.done)
                if b.later:
                    pe.wait_ge(rl2_ready, b.before)
                transposed(b, NC, bank_c, ncT_psum)

            def cmix_up(b, n):
                pe.wait_ge(xk2_ready if n == 0 else kr_ready[n - 1], b.done)
                t_.matmul(bank_c[:], FWk[:, n * P:(n + 1) * P], XK2[:], start=True, stop=True).then_inc(kk_psum[n], 1)

            def cmix_down(b, n):
                pe.wait_ge(kk_ready[n], b.done)
                if n == 0:
                    if b.later:
                        pe.wait_ge(kvs_ready, b.before)
                for j in range(J):
                    last = t_.matmul(bank_kv[:, j * C:(j + 1) * C], KK[:, n, j * P:(j + 1) * P], FWv[:, n, :],
                                     start=(n == 0 and j == 0), stop=(n == H - 1), skip_group_check=True)
                if n == H - 1:
                    last.then_inc(kv_psum, 1)

            def cmix_r(b):
                pe.wait_ge(xr2_ready, b.done)
                pe.wait_ge(kr_ready[H - 1], b.done)
                for j in range(J):
                    last = t_.matmul(bank_c[:, j * C:(j + 1) * C], XR2[:, j * P:(j + 1) * P], FWr[:], start=True, stop=True)
                last.then_inc(r2_psum, 1)

            behind = STAGES - 1

            def iteration(h, t, c, g):
                if g is not None:
                    ffn_transpose(g, f2, f1, g.turn(behind))
                if c is not None:
                    cmix_transpose(c)
                if t is not None:
                    tmix_transpose(t)
                if h is not None:
                    attn_transpose(h)
                if g is not None:
                    ffn_hidden(g, f2, 0)
                    ffn_start(g, f2, f1, g.turn(behind))
                    ffn_hidden(g, f2, 1)
                    ffn_down(g, f2, 0)
                if h is not None:
                    attn_gram(h)
                if c is not None:
                    cmix_up(c, 0)
                if t is not None:
                    tmix_product(t, XK, xk_ready, Wk, bank_k, k_psum, None)
                if h is not None:
                    attn_proj(h)
                if g is not None:
                    ffn_hidden(g, f2, 2)
                    ffn_down(g, f2, 1)
                if t is not None:
                    tmix_product(t, XV, xv_ready, Wv, bank_v, v_psum, m2_ready)
                    tmix_product(t, XR, xr_ready, Wr, bank_r, r_psum, rl_ready)
                if h is not None:
                    attn_apply(h)
                if g is not None:
                    ffn_hidden(g, f2, 3)
                    ffn_down(g, f2, 2)
                    ffn_down(g, f2, 3)
                if h is not None:
                    ffn_transpose(h, f1, f2, h.turn(1 - behind))
                if c is not None:
                    for n in range(1, H):
                        cmix_up(c, n)
                        cmix_down(c, n - 1)
                    cmix_r(c)
                    cmix_down(c, H - 1)
                if h is not None:
                    ffn_hidden(h, f1, 0)
                    ffn_start(h, f1, f2, h.turn(1 - behind))
                    for n in range(1, H):
                        ffn_hidden(h, f1, n)
                        ffn_down(h, f1, n - 1)
                    ffn_down(h, f1, H - 1)
                if t is not None:
                    tmix_o(t)

            pe.wait_ge(ident_ready, 1)
            pe.wait_ge(loaded["first"], 32)
            pe.wait_ge(loaded["ffn"], 80)
            pe.wait_ge(loaded["tmix"], 64)
            pe.wait_ge(loaded["cmix"], 48)
            each_iteration(pe, iteration)


def kernel(**inputs):
    import numpy as np
    import concourse.bacc as bacc
    from concourse.bass_utils import run_bass_kernel_spmd

    get = {n: np.asarray(a) for n, a in inputs.items()}
    rw = {n[len("L0_attn_b_"):]: a for n, a in get.items() if n.startswith("L0_attn_b_")}
    ffn = {n[len("L0_ffn_"):]: a for n, a in get.items() if n.startswith("L0_ffn_")}
    hidden = get["L0_attn_a_hidden_states"]
    C = hidden.shape[2]
    J = hidden.shape[1] // P
    vectors = {"ln1_g": rw["ln1_g"], "ln1_b": rw["ln1_b"], "ln2_g": rw["ln2_g"], "ln2_b": rw["ln2_b"],
               "decay": rw["time_decay"], "first": rw["time_first"], "mix_k": rw["time_mix_k"],
               "mix_v": rw["time_mix_v"], "mix_r": rw["time_mix_r"], "cm_k": rw["cm_k"], "cm_r": rw["cm_r"],
               "b2": ffn["b2"][0]}
    laid = {
        "hidden": hidden, "w_q": get["L0_attn_a_W_q"],
        "w1": ffn["w1"][0], "w2": ffn["w2"][0], "b1": ffn["b1"][0].reshape(-1, P).T,
        "wk": rw["att_Wk"].T, "wv": rw["att_Wv"].T, "wr": rw["att_Wr"].T, "wo": rw["att_Wo"].T,
        "f_wk": rw["ffn_Wk"].T, "f_wr": rw["ffn_Wr"].T, "f_wv": rw["ffn_Wv"].T,
        "vectors": np.stack([vectors[n] for n in VECTORS], axis=1),
        "gamma": np.tile(ffn["gamma"], (P, 1)), "beta": np.tile(ffn["beta"], (P, J)),
    }
    nc = bacc.Bacc("TRN2", target_bir_lowering=False, num_devices=1)
    arrays, args = {}, []
    for name, a in laid.items():
        a = np.ascontiguousarray(a)
        arrays["in_" + name] = a
        args.append(nc.dram_tensor("in_" + name, a.shape, mybir.dt.from_np(a.dtype), kind="ExternalInput").ap())
    args.append(nc.dram_tensor("out_x", hidden.shape, F32, kind="ExternalOutput").ap())
    hybrid_layer(nc, *args)
    return run_bass_kernel_spmd(nc, [arrays], core_ids=[0]).results[0]["out_x"]
```

```python
from contextlib import ExitStack

import concourse.bass as bass
from concourse import mybir
from concourse.alu_op_type import AluOpType as ALU

F32 = mybir.dt.float32
ACT = mybir.ActivationFunctionType

P = 128
EPS = 1e-5
MIN_LOG = -1e38
STAGES = 4
DMA = 16

VECTORS = ["ln1_g", "ln1_b", "ln2_g", "ln2_b", "decay", "first", "mix_k", "mix_v", "mix_r", "cm_k", "cm_r", "b2"]


class At:

    def __init__(self, values, offset, active=True):
        self.values, self.offset, self.active = values, offset, active
        self.done, self.before = values[1][offset + 1], values[1][offset]
        self.looped = not isinstance(self.before, int)
        self.later = self.looped or self.before > 0

    def count(self, more=0, each=1):
        return self.values[each][self.offset + more]

    def freed(self, users):
        return users[:1] if self.looped else [(s, n) for s, n in users if n > 0]


def step(program):
    def run(b, *args, **more):
        if b.active:
            program(b, *args, **more)
    return run


def hybrid_layer(nc, hidden, w_q, w1, w2, b1, wk, wv, wr, wo, f_wk, f_wr, f_wv, vectors, gamma, beta, out):
    B, T, C = hidden.shape
    J = T // P
    H = w1.shape[1] // P
    assert C == P and f_wk.shape[1] == H * P

    with ExitStack() as ctx:
        def sb(name, shape):
            return ctx.enter_context(nc.sbuf_tensor(name, shape, F32))

        def sem(name):
            return ctx.enter_context(nc.semaphore(name))

        def rows(name):
            return sb(name, [P, J, P])

        def cols(name):
            return sb(name, [P, T])

        Wq = sb("Wq", [P, C])
        W1 = sb("W1", [P, H * P])
        W2 = sb("W2", [P, H, C])
        Wk, Wv, Wr, Wo, FWr = (sb(n, [P, C]) for n in ("Wk", "Wv", "Wr", "Wo", "FWr"))
        FWk = sb("FWk", [P, H * P])
        FWv = sb("FWv", [P, H, C])
        B1 = sb("B1", [P, H])
        VEC = sb("VEC", [P, len(VECTORS)])
        GAMMA = sb("GAMMA", [P, C])
        BETA = sb("BETA", [P, J, C])
        IDENT = sb("IDENT", [P, P])
        ONE = sb("ONE", [P, 1])
        WDEC = sb("WDEC", [P, 1])
        WEXP = sb("WEXP", [P, 1])
        WROW = sb("WROW", [P, T])
        K_EPS, K_NEG, K_RSQRT = (sb(n, [P, 2 * J]) for n in ("K_EPS", "K_NEG", "K_RSQRT"))

        def vec(name):
            n = VECTORS.index(name)
            return VEC[:, n:n + 1]

        banks = [ctx.enter_context(nc.psum_tensor(f"bank{n}", [P, T], F32)) for n in range(8)]
        bank_aT, bank_aG, bank_aP, bank_aA = banks[3], banks[1], banks[2], banks[4]
        bank_tT, bank_k, bank_v, bank_r, bank_o = banks[6], banks[2], banks[1], banks[3], banks[1]
        bank_cT, bank_r2, bank_kv = banks[6], banks[6], banks[0]
        bank_kk = [banks[2], banks[5], banks[1], banks[4]]
        f1_banks = {"T": banks[7], "h": [banks[4], banks[5], banks[6], banks[2]], "z": banks[7]}
        f2_banks = {"T": banks[5], "h": [banks[3], banks[4], banks[6], banks[2]], "z": banks[7]}
        loaded = {n: sem("loaded_" + n) for n in ("first", "ffn", "tmix", "cmix")}
        const_ready = sem("const_ready")
        ident_ready = sem("ident_ready")
        decay_exp, decay_ready, decay_row = sem("decay_exp"), sem("decay_ready"), sem("decay_row")
        pads_ready = sem("pads_ready")

        class Norm:

            def __init__(self, n, kind="plain"):
                self.stats = sb(n + "_stats", [P, J, 6])
                self.mv = sb(n + "_mv", [P, J, 2])
                self.ve = sb(n + "_ve", [P, 2 * J])
                self.tmp = sb(n + "_tmp", [P, J])
                self.carry = sb(n + "_carry", [P, 1])
                self.nm = sb(n + "_nm", [P, J])
                self.rs = sb(n + "_rs", [P, 2 * J])
                self.nb = sb(n + "_nb", [P, J])
                self.back = sb(n + "_back", [P, J])
                self.stats_done = sem(n + "_stats_done")
                self.mv_ready = sem(n + "_mv_ready")
                self.ve_ready = sem(n + "_ve_ready")
                self.rs_ready = sem(n + "_rs_ready")
                if kind != "scale only":
                    self.nb_ready = sem(n + "_nb_ready")
                if kind == "twice":
                    self.tmp_ready = sem(n + "_tmp_ready")
                    self.q_ready = sem(n + "_q_ready")

        class Ffn:

            def __init__(self, n, x, x_ready, y_out, out_used, banks):
                self.bank_T, self.bank_h, self.bank_z = banks["T"], banks["h"], banks["z"]
                self.z_rows = self.bank_z[:].rearrange("p (j c) -> p j c", j=J)
                self.x, self.x_ready = x, x_ready
                self.norm, self.znorm = Norm(n + "_y"), Norm(n + "_z", "scale only")
                self.xb, self.xb_ready = rows(n + "_xb"), sem(n + "_xb_ready")
                self.y, self.y_ready = rows(n + "_y"), sem(n + "_y_ready")
                self.yT_psum, self.yT_ready = sem(n + "_yT_psum"), sem(n + "_yT_ready")
                self.yT = cols(n + "_yT")
                self.yTb, self.yTb_ready = cols(n + "_yTb"), sem(n + "_yTb_ready")
                self.h = sb(n + "_h", [P, H, T])
                self.h_psum = [sem(f"{n}_h{f}_psum") for f in range(H)]
                self.h_ready = [sem(f"{n}_h{f}_ready") for f in range(H)]
                self.z_psum = sem(n + "_z_psum")
                self.zg, self.zg_ready = rows(n + "_zg"), sem(n + "_zg_ready")
                self.out, self.out_ready = y_out, sem(n + "_out_ready")
                self.out_used = out_used

        X0, x0_loaded = rows("X0"), sem("x0_loaded")
        na = Norm("attn")
        XN, xn_ready = rows("XN"), sem("xn_ready")
        xnT_psum, xnT_ready = sem("xnT_psum"), sem("xnT_ready")
        XNT = cols("XNT")
        GRAM, gram_psum, gram_ready = sb("GRAM", [P, C]), sem("gram_psum"), sem("gram_ready")
        PROJ, proj_psum, proj_ready = sb("PROJ", [P, C]), sem("proj_psum"), sem("proj_ready")
        attn_psum = sem("attn_psum")
        X1, x1_ready = rows("X1"), sem("x1_ready")
        X2, X3, X4 = rows("X2"), rows("X3"), rows("X4")

        x2_kept = sem("x2_kept")
        stored = sem("stored")
        nt = Norm("tmix", "twice")
        X2K = rows("X2K")
        back_half, back_ready = sem("back_half"), sem("back_ready")
        N, n_ready = rows("N"), sem("n_ready")
        nT_psum = sem("nT_psum")
        XA, xa_ready = sb("XA", [P, T + 1]), sem("xa_ready")
        DX, dx_ready = cols("DX"), sem("dx_ready")
        XK, xk_ready = cols("XK"), sem("xk_ready")
        XV, xv_ready = cols("XV"), sem("xv_ready")
        XR, xr_ready = cols("XR"), sem("xr_ready")
        k_psum, v_psum, r_psum = sem("k_psum"), sem("v_psum"), sem("r_psum")
        PP, pp_ready = sb("PP", [P, T + 1]), sem("pp_ready")
        DIFF, diff_ready = sb("DIFF", [P, 2, T]), sem("diff_ready")
        LOW, low_ready = sb("LOW", [P, 2, T]), sem("low_ready")
        HIGH, high_ready = sb("HIGH", [P, 2, T]), sem("high_ready")
        EA, ea_ready = sb("EA", [P, 3, T]), sem("ea_ready")
        EB, eb_ready = sb("EB", [P, 2, T]), sem("eb_ready")
        EV, ev_ready = cols("EV"), sem("ev_ready")
        AB, ab_ready, b_ready = sb("AB", [P, 2, T + 1]), sem("ab_ready"), sem("b_ready")
        m2_ready = sem("m2_ready")
        M1, m1_ready = sb("M1", [P, 2, T]), sem("m1_ready")
        ND, nd_ready = sb("ND", [P, 2, T]), sem("nd_ready")
        AR, ar_ready = cols("AR"), sem("ar_ready")
        ER, er_ready = cols("ER"), sem("er_ready")
        DN, dn_ready = cols("DN"), sem("dn_ready")
        LD, ld_ready = cols("LD"), sem("ld_ready")
        RL, rl_ready = cols("RL"), sem("rl_ready")
        RC, rc_ready = cols("RC"), sem("rc_ready")
        RW, rw_ready = cols("RW"), sem("rw_ready")
        o_psum = sem("o_psum")
        U1, u1_ready = rows("U1"), sem("u1_ready")
        X2U, x2u_ready = rows("X2U"), sem("x2u_ready")

        ncm = Norm("cmix")
        NC, nc_ready = rows("NC"), sem("nc_ready")
        ncT_psum = sem("ncT_psum")
        XC, xc_ready = sb("XC", [P, T + 1]), sem("xc_ready")
        DC, dc_ready = cols("DC"), sem("dc_ready")
        XK2, xk2_ready = cols("XK2"), sem("xk2_ready")
        XR2, xr2_ready = cols("XR2"), sem("xr2_ready")
        kk_psum = [sem(f"kk{f}_psum") for f in range(H)]
        KR, kr_ready = sb("KR", [P, H, T]), [sem(f"kr{f}_ready") for f in range(H)]
        KK, kk_ready = sb("KK", [P, H, T]), [sem(f"kk{f}_ready") for f in range(H)]
        kv_psum, r2_psum = sem("kv_psum"), sem("r2_psum")
        AR2, ar2_ready = cols("AR2"), sem("ar2_ready")
        ER2, er2_ready = cols("ER2"), sem("er2_ready")
        LD2, ld2_ready = cols("LD2"), sem("ld2_ready")
        RL2, rl2_ready = cols("RL2"), sem("rl2_ready")
        SG, sg_ready = cols("SG"), sem("sg_ready")
        KVS, kvs_ready = cols("KVS"), sem("kvs_ready")
        x3_ready = sem("x3_ready")

        f1 = Ffn("f1", X1, x1_ready, X2, [(x2_kept, DMA), (n_ready, 1)], f1_banks)
        f2 = Ffn("f2", X3, x3_ready, X4, [(stored, DMA)], f2_banks)
        x2_ready, x4_ready = f1.out_ready, f2.out_ready

        def each_iteration(engines, body, after_first=None, dma_counts=()):
            first, last = STAGES, B
            stages = lambda values, i: [
                At(values, -s, i is None or 0 <= i - s < B) for s in range(STAGES)]
            span = range(-STAGES, 2)

            def numbers(i):
                return {each: {k: max(0, min(i + k, B)) * each for k in span} for each in (1, DMA)}

            for i in range(first):
                body(*stages(numbers(i), i))
                if i == 0 and after_first is not None:
                    after_first()
            with engines.Fori(first, last) as i:
                def held(value, name):
                    register = engines.alloc_register(name)
                    engines.reg_mov(register, value)
                    return engines.snap(register)

                registers = {1: {k: held(i + k, f"n{k + STAGES}") for k in range(-STAGES + 1, 2)}}
                registers[DMA] = {k: held((i + k) * DMA, f"dma{k + STAGES}") for k in dma_counts}
                body(*stages(registers, None))
            for i in range(last, B + STAGES - 1):
                body(*stages(numbers(i), i))

        block = ctx.enter_context(nc.Block())

        @block.sync
        def _(sp):
            x0_dram = hidden.rearrange("b t c -> (b t) c")
            out_dram = out.rearrange("b t c -> (b t) c")

            @step
            def load_x0(b):
                if b.later:
                    sp.wait_ge(x1_ready, b.before)
                sp.dma_start(X0[:], of(x0_dram, b)).then_inc(x0_loaded, DMA)

            @step
            def keep_x2(b):
                sp.wait_ge(x2_ready, b.done)
                if b.later:
                    sp.wait_ge(x2u_ready, b.before)
                sp.dma_start(X2K[:], X2[:]).then_inc(x2_kept, DMA)

            @step
            def store(b):
                sp.wait_ge(x4_ready, b.done)
                sp.dma_start(of(out_dram, b), X4[:]).then_inc(stored, DMA)

            def of(dram, b):
                return dram[bass.ds(b.count() * T, T), :].rearrange("(j p) c -> p j c", p=P)

            def iteration(s0, s1, s2, s3):
                load_x0(s0)
                keep_x2(s1)
                store(s3)

            def weights():
                sp.dma_start(Wq[:], w_q).then_inc(loaded["first"], 16)
                sp.dma_start(VEC[:], vectors).then_inc(loaded["first"], 16)
                sp.dma_start(W1[:], w1).then_inc(loaded["ffn"], 16)
                sp.dma_start(B1[:], b1).then_inc(loaded["ffn"], 16)
                sp.dma_start(W2[:], w2.rearrange("(f p) c -> p f c", p=P)).then_inc(loaded["ffn"], 16)
                sp.dma_start(GAMMA[:], gamma).then_inc(loaded["ffn"], 16)
                sp.dma_start(BETA[:].rearrange("p j c -> p (j c)"), beta).then_inc(loaded["ffn"], 16)
                for t, d in ((Wk, wk), (Wv, wv), (Wr, wr), (Wo, wo)):
                    sp.dma_start(t[:], d).then_inc(loaded["tmix"], 16)
                sp.dma_start(FWk[:], f_wk).then_inc(loaded["cmix"], 16)
                sp.dma_start(FWr[:], f_wr).then_inc(loaded["cmix"], 16)
                sp.dma_start(FWv[:], f_wv.rearrange("(f p) c -> p f c", p=P)).then_inc(loaded["cmix"], 16)

            each_iteration(sp, iteration, after_first=weights)
            sp.wait_ge(stored, DMA * B)

        @block.gpsimd
        def _(pool):
            pool.memset(K_EPS[:], EPS).then_inc(const_ready, 1)
            pool.memset(K_NEG[:], -1.0).then_inc(const_ready, 1)
            pool.memset(K_RSQRT[:], -0.5).then_inc(const_ready, 1)
            pool.memset(ONE[:], 1.0).then_inc(const_ready, 1)
            pool.memset(IDENT[:], 0.0).then_inc(const_ready, 1)
            pool.wait_ge(const_ready, 5)
            pool.affine_select(out=IDENT[:], in_=IDENT[:], compare_op=ALU.not_equal, fill=1.0, base=0,
                               pattern=[[-1, P]], channel_multiplier=1).then_inc(ident_ready, 1)
            pool.memset(XA[:, 0:1], 0.0).then_inc(pads_ready, 1)
            pool.memset(XC[:, 0:1], 0.0).then_inc(pads_ready, 1)
            pool.memset(AB[:, :, 0:1], 0.0).then_inc(pads_ready, 1)
            pool.memset(PP[:, 0:1], MIN_LOG).then_inc(pads_ready, 1)

            @step
            def scale(b, n, users, with_bias=True):
                pool.wait_ge(n.mv_ready, b.done)
                for s in users:
                    if b.later:
                        pool.wait_ge(s, b.before)
                if with_bias:
                    pool.tensor_tensor(n.nm[:], n.mv[:, :, 0], K_NEG[:, 0:J], ALU.mult)
                pool.tensor_tensor(n.ve[:, 0:J], n.mv[:, :, 1], K_EPS[:, 0:J], ALU.add).then_inc(n.ve_ready, 1)
                pool.wait_ge(n.ve_ready, b.done)
                pool.tensor_tensor(n.rs[:, 0:J], n.ve[:, 0:J], K_RSQRT[:, 0:J], ALU.pow).then_inc(n.rs_ready, 1)
                if with_bias:
                    pool.wait_ge(n.rs_ready, b.done)
                    pool.tensor_tensor(n.nb[:], n.nm[:], n.rs[:, 0:J], ALU.mult).then_inc(n.nb_ready, 1)

            @step
            def scale_twice(b, n):
                pool.wait_ge(n.mv_ready, b.done)
                if b.later:
                    pool.wait_ge(back_ready, b.before)
                if b.later:
                    pool.wait_ge(n_ready, b.before)
                pool.tensor_tensor(n.nm[:], n.mv[:, :, 0], K_NEG[:, 0:J], ALU.mult)
                pool.tensor_tensor(n.ve[:, J:], n.mv[:, :, 1], K_EPS[:, 0:J], ALU.add).then_inc(n.ve_ready, 1)
                pool.wait_ge(n.ve_ready, b.done)
                pool.tensor_tensor(n.tmp[:], n.ve[:, J:], K_EPS[:, 0:J], ALU.mult).then_inc(n.tmp_ready, 1)
                pool.wait_ge(n.tmp_ready, b.done)
                pool.tensor_tensor(n.ve[:, 0:J], n.mv[:, :, 1], n.tmp[:], ALU.add).then_inc(n.q_ready, 1)
                pool.wait_ge(n.q_ready, b.done)
                pool.tensor_tensor(n.rs[:], n.ve[:], K_RSQRT[:], ALU.pow).then_inc(n.rs_ready, 1)
                pool.wait_ge(n.rs_ready, b.done)
                pool.tensor_tensor(n.nb[:], n.nm[:], n.rs[:, 0:J], ALU.mult).then_inc(n.nb_ready, 1)

            @step
            def back_scale(b, n):
                pool.wait_ge(n.rs_ready, b.done)
                if b.later:
                    pool.wait_ge(u1_ready, b.before)
                pool.tensor_tensor(n.tmp[:], n.ve[:, 0:J], n.rs[:, 0:J], ALU.mult).then_inc(back_half, 1)
                pool.wait_ge(back_half, b.done)
                pool.tensor_tensor(n.back[:], n.tmp[:], n.rs[:, J:], ALU.mult).then_inc(back_ready, 1)

            def iteration(s0, s1, s2, s3):
                scale(s0, na, [xn_ready])
                scale(s3, f2.norm, [f2.y_ready])
                scale(s1, f1.znorm, [f1.out_ready], with_bias=False)
                scale(s2, ncm, [nc_ready])
                scale_twice(s1, nt)
                back_scale(s1, nt)
                scale(s0, f1.norm, [f1.y_ready])
                scale(s3, f2.znorm, [f2.out_ready], with_bias=False)

            each_iteration(pool, iteration)

        @block.vector
        def _(dve):
            v = nc.vector

            @step
            def stats(b, n, src, src_ready, each=1):
                dve.wait_ge(src_ready, b.count(1, each))
                if b.later:
                    dve.wait_ge(n.mv_ready, b.before)
                for j in range(J):
                    last = v.bn_stats(n.stats[:, j, :], src[:, j, :])
                last.then_inc(n.stats_done, 1)

            @step
            def mean_var(b, n, scale_ready):
                if b.later:
                    dve.wait_ge(scale_ready, b.before)
                dve.wait_ge(n.stats_done, b.done)
                v.memset(n.carry[:], 0.0)
                for j in range(J):
                    last = v.bn_aggr(n.mv[:, j, :], n.stats[:, j, :])
                last.then_inc(n.mv_ready, 1)

            @step
            def attn_out(b):
                dve.wait_ge(attn_psum, b.done)
                if b.later:
                    dve.wait_ge(f1.y_ready, b.before)
                if b.later:
                    dve.wait_ge(f1.xb_ready, b.before)
                v.tensor_tensor(X1[:], bank_aA[:].rearrange("p (j c) -> p j c", j=J), X0[:], ALU.add).then_inc(x1_ready, 1)

            @step
            def ffn_residual(b, f):
                dve.wait_ge(f.x_ready, b.done)
                if b.later:
                    dve.wait_ge(f.out_ready, b.before)
                v.tensor_tensor(f.xb[:], f.x[:], BETA[:], ALU.add).then_inc(f.xb_ready, 1)

            @step
            def ffn_gain(b, f):
                dve.wait_ge(f.znorm.mv_ready, b.done)
                if b.later:
                    dve.wait_ge(f.out_ready, b.before)
                for j in range(J):
                    last = v.scalar_tensor_tensor(f.zg[:, j, :], f.z_rows[:, j, :], f.znorm.mv[:, j, 0:1], GAMMA[:],
                                                  ALU.subtract, ALU.mult)
                last.then_inc(f.zg_ready, 1)

            @step
            def ffn_out(b, f):
                dve.wait_ge(f.znorm.rs_ready, b.done)
                dve.wait_ge(f.zg_ready, b.done)
                dve.wait_ge(f.xb_ready, b.done)
                for s, each in f.out_used:
                    if b.later:
                        dve.wait_ge(s, b.count(0, each))
                for j in range(J):
                    last = v.scalar_tensor_tensor(f.out[:, j, :], f.zg[:, j, :], f.znorm.rs[:, j:j + 1], f.xb[:, j, :],
                                                  ALU.mult, ALU.add)
                last.then_inc(f.out_ready, 1)

            @step
            def change(b, x, x_ready, diff, diff_ready, diff_used):
                dve.wait_ge(x_ready, b.done)
                for s in diff_used:
                    if b.later:
                        dve.wait_ge(s, b.before)
                v.tensor_tensor(diff[:], x[:, 1:], x[:, 0:T], ALU.subtract).then_inc(diff_ready, 1)

            @step
            def mix(b, x, diff, diff_ready, weight, dst, dst_ready, dst_used):
                dve.wait_ge(diff_ready, b.done)
                if b.later:
                    dve.wait_ge(dst_used, b.before)
                v.scalar_tensor_tensor(dst[:], diff[:], vec(weight), x[:, 0:T], ALU.mult, ALU.add).then_inc(dst_ready, 1)

            @step
            def running_max(b):
                dve.wait_ge(k_psum, b.done)
                if b.later:
                    dve.wait_ge(diff_ready, b.before)
                v.tensor_tensor_scan(PP[:, 1:], WROW[:], bank_k[:], MIN_LOG, ALU.add, ALU.max).then_inc(pp_ready, 1)

            @step
            def differences(b):
                dve.wait_ge(pp_ready, b.done)
                if b.later:
                    dve.wait_ge(low_ready, b.before)
                if b.later:
                    dve.wait_ge(high_ready, b.before)
                v.scalar_tensor_tensor(DIFF[:, 0, :], PP[:, 0:T], WDEC[:], bank_k[:], ALU.add, ALU.subtract)
                v.scalar_tensor_tensor(DIFF[:, 1, :], bank_k[:], vec("first"), PP[:, 0:T],
                                       ALU.add, ALU.subtract).then_inc(diff_ready, 1)

            @step
            def exponents_low(b):
                dve.wait_ge(diff_ready, b.done)
                if b.later:
                    dve.wait_ge(ea_ready, b.before)
                v.tensor_scalar(LOW[:], DIFF[:], 0.0, None, ALU.min).then_inc(low_ready, 1)

            @step
            def exponents_high(b):
                dve.wait_ge(diff_ready, b.done)
                if b.later:
                    dve.wait_ge(eb_ready, b.before)
                v.tensor_scalar(HIGH[:], DIFF[:], 0.0, None, ALU.max).then_inc(high_ready, 1)

            @step
            def new_values(b):
                dve.wait_ge(eb_ready, b.done)
                dve.wait_ge(v_psum, b.done)
                if b.later:
                    dve.wait_ge(ab_ready, b.before)
                v.tensor_tensor(EV[:], EB[:, 0, :], bank_v[:], ALU.mult).then_inc(ev_ready, 1)

            @step
            def first_values(b):
                dve.wait_ge(ea_ready, b.done)
                dve.wait_ge(v_psum, b.done)
                if b.later:
                    dve.wait_ge(nd_ready, b.before)
                v.tensor_tensor(EA[:, 1, :], EA[:, 2, :], bank_v[:], ALU.mult).then_inc(m2_ready, 1)

            @step
            def denominator_sum(b):
                dve.wait_ge(ea_ready, b.done)
                dve.wait_ge(eb_ready, b.done)
                if b.later:
                    dve.wait_ge(m1_ready, b.before)
                v.tensor_tensor_scan(AB[:, 1, 1:], EA[:, 0, :], EB[:, 0, :], 0.0, ALU.mult, ALU.add).then_inc(b_ready, 1)

            @step
            def numerator_sum(b):
                dve.wait_ge(ev_ready, b.done)
                dve.wait_ge(ea_ready, b.done)
                if b.later:
                    dve.wait_ge(m1_ready, b.before)
                v.tensor_tensor_scan(AB[:, 0, 1:], EA[:, 0, :], EV[:], 0.0, ALU.mult, ALU.add).then_inc(ab_ready, 1)

            @step
            def weighted(b):
                dve.wait_ge(b_ready, b.done)
                dve.wait_ge(ab_ready, b.done)
                if b.later:
                    dve.wait_ge(nd_ready, b.before)
                v.tensor_tensor(M1[:], AB[:, :, 0:T], EB[:, 1:2, :].broadcast_to([P, 2, T]), ALU.mult).then_inc(m1_ready, 1)

            @step
            def with_current(b):
                dve.wait_ge(m1_ready, b.done)
                dve.wait_ge(m2_ready, b.done)
                if b.later:
                    dve.wait_ge(rw_ready, b.before)
                if b.later:
                    dve.wait_ge(dn_ready, b.before)
                v.tensor_tensor(ND[:], M1[:], EA[:, 1:3, :], ALU.add).then_inc(nd_ready, 1)

            @step
            def gate_sum(b):
                dve.wait_ge(nd_ready, b.done)
                dve.wait_ge(er_ready, b.done)
                if b.later:
                    dve.wait_ge(ld_ready, b.before)
                v.scalar_tensor_tensor(DN[:], ER[:], 1.0, ND[:, 1, :], ALU.add, ALU.mult).then_inc(dn_ready, 1)

            @step
            def gate_log(b):
                dve.wait_ge(ld_ready, b.done)
                if b.later:
                    dve.wait_ge(rc_ready, b.before)
                v.scalar_tensor_tensor(RL[:], bank_r[:], 0.0, LD[:], ALU.min, ALU.subtract).then_inc(rl_ready, 1)

            @step
            def gated(b):
                dve.wait_ge(rc_ready, b.done)
                if b.later:
                    dve.wait_ge(o_psum, b.before)
                v.tensor_tensor(RW[:], ND[:, 0, :], RC[:], ALU.mult).then_inc(rw_ready, 1)

            @step
            def tmix_out(b):
                dve.wait_ge(o_psum, b.done)
                dve.wait_ge(back_ready, b.done)
                if b.later:
                    dve.wait_ge(nc_ready, b.before)
                if b.later:
                    dve.wait_ge(x2u_ready, b.before)
                o = bank_o[:].rearrange("p (j c) -> p j c", j=J)
                for j in range(J):
                    last = v.scalar_tensor_tensor(U1[:, j, :], N[:, j, :], nt.back[:, j:j + 1], o[:, j, :],
                                                  ALU.mult, ALU.add)
                last.then_inc(u1_ready, 1)

            @step
            def tmix_residual(b):
                dve.wait_ge(u1_ready, b.done)
                dve.wait_ge(x2_kept, b.count(1, DMA))
                if b.later:
                    dve.wait_ge(x3_ready, b.before)
                v.tensor_tensor(X2U[:], X2K[:], U1[:], ALU.add).then_inc(x2u_ready, 1)

            @step
            def cgate_log(b):
                dve.wait_ge(ld2_ready, b.done)
                if b.later:
                    dve.wait_ge(sg_ready, b.before)
                v.scalar_tensor_tensor(RL2[:], bank_r2[:], 0.0, LD2[:], ALU.min, ALU.subtract).then_inc(rl2_ready, 1)

            @step
            def cmix_gated(b):
                dve.wait_ge(sg_ready, b.done)
                dve.wait_ge(kv_psum, b.done)
                if b.later:
                    dve.wait_ge(x3_ready, b.before)
                v.tensor_tensor(KVS[:], bank_kv[:], SG[:], ALU.mult).then_inc(kvs_ready, 1)

            @step
            def cmix_out(b):
                dve.wait_ge(kvs_ready, b.done)
                dve.wait_ge(x2u_ready, b.done)
                if b.later:
                    dve.wait_ge(f2.y_ready, b.before)
                if b.later:
                    dve.wait_ge(f2.xb_ready, b.before)
                v.tensor_tensor(X3[:], KVS[:].rearrange("p (j c) -> p j c", j=J), X2U[:], ALU.add).then_inc(x3_ready, 1)

            def iteration(s0, s1, s2, s3):
                running_max(s2)
                differences(s2)
                cgate_log(s3)
                exponents_high(s2)
                exponents_low(s2)
                stats(s0, na, X0, x0_loaded, each=DMA)
                cmix_gated(s3)
                mean_var(s0, na, na.nb_ready)
                cmix_out(s3)
                new_values(s2)
                stats(s3, f2.norm, X3, f2.x_ready)
                denominator_sum(s2)
                numerator_sum(s2)
                mean_var(s3, f2.norm, f2.norm.nb_ready)
                first_values(s2)
                weighted(s2)
                with_current(s2)
                gate_sum(s2)
                stats(s1, f1.znorm, f1.z_rows, f1.z_psum)
                gate_log(s2)
                mean_var(s1, f1.znorm, f1.znorm.rs_ready)
                ffn_residual(s1, f1)
                gated(s2)
                ffn_gain(s1, f1)
                tmix_out(s2)
                stats(s2, ncm, U1, u1_ready)
                mean_var(s2, ncm, ncm.nb_ready)
                ffn_out(s1, f1)
                stats(s1, nt, X2, x2_ready)
                mean_var(s1, nt, back_ready)
                ffn_residual(s3, f2)
                attn_out(s0)
                tmix_residual(s2)
                stats(s0, f1.norm, X1, f1.x_ready)
                change(s2, XC, xc_ready, DC, dc_ready, [xk2_ready, xr2_ready])
                mix(s2, XC, DC, dc_ready, "cm_k", XK2, xk2_ready, kk_psum[H - 1])
                stats(s3, f2.znorm, f2.z_rows, f2.z_psum)
                mix(s2, XC, DC, dc_ready, "cm_r", XR2, xr2_ready, r2_psum)
                mean_var(s3, f2.znorm, f2.znorm.rs_ready)
                mean_var(s0, f1.norm, f1.norm.nb_ready)
                ffn_gain(s3, f2)
                change(s1, XA, xa_ready, DX, dx_ready, [xk_ready, xv_ready, xr_ready])
                mix(s1, XA, DX, dx_ready, "mix_k", XK, xk_ready, k_psum)
                mix(s1, XA, DX, dx_ready, "mix_r", XR, xr_ready, r_psum)
                mix(s1, XA, DX, dx_ready, "mix_v", XV, xv_ready, v_psum)
                ffn_out(s3, f2)

            dve.wait_ge(loaded["first"], 32)
            dve.wait_ge(decay_ready, 1)
            v.memset(WROW[:], 0.0).then_inc(decay_row, 1)
            dve.wait_ge(decay_row, 1)
            v.tensor_scalar(WROW[:], WROW[:], WDEC[:], None, ALU.add).then_inc(decay_row, 1)
            dve.wait_ge(decay_row, 2)
            dve.wait_ge(pads_ready, 4)
            dve.wait_ge(loaded["ffn"], 80)
            each_iteration(dve, iteration, dma_counts=(1, -1, -3))

        @block.scalar
        def _(act):
            a = nc.scalar

            @step
            def normed(b, n, src, dst, dst_ready, dst_used):
                act.wait_ge(n.nb_ready, b.done)
                for s in dst_used:
                    if b.later:
                        act.wait_ge(s, b.before)
                for j in range(J):
                    last = a.activation(dst[:, j, :], src[:, j, :], ACT.Identity, scale=n.rs[:, j:j + 1], bias=n.nb[:, j:j + 1])
                last.then_inc(dst_ready, 1)

            @step
            def evacuate(b, src, src_ready, dst, dst_ready, dst_used):
                act.wait_ge(src_ready, b.done)
                for s in dst_used:
                    if b.later:
                        act.wait_ge(s, b.before)
                a.activation(dst, src, ACT.Copy).then_inc(dst_ready, 1)

            @step
            def evacuate_affine(b, src_ready, bank, dst, gain, shift, dst_ready, dst_used):
                act.wait_ge(src_ready, b.done)
                for s in dst_used:
                    if b.later:
                        act.wait_ge(s, b.before)
                a.activation(dst[:, 1:], bank[:], ACT.Identity, scale=vec(gain), bias=vec(shift)).then_inc(dst_ready, 1)

            @step
            def ffn_y_bias(b, f):
                act.wait_ge(f.yT_psum, b.done)
                if b.later:
                    act.wait_ge(f.z_psum, b.before)
                a.activation(f.yTb[:], f.bank_T[:], ACT.Identity, bias=vec("b2")).then_inc(f.yTb_ready, 1)

            @step
            def ffn_relu(b, f, n):
                act.wait_ge(f.h_psum[n], b.done)
                if b.later:
                    act.wait_ge(f.z_psum, b.before)
                a.activation(f.h[:, n, :], f.bank_h[n][:], ACT.Relu, bias=B1[:, n:n + 1]).then_inc(f.h_ready[n], 1)

            @step
            def exp_low(b):
                act.wait_ge(low_ready, b.done)
                if b.later:
                    act.wait_ge(nd_ready, b.before)
                a.activation(EA[:, 0:3:2, :], LOW[:], ACT.Exp).then_inc(ea_ready, 1)

            @step
            def exp_high(b):
                act.wait_ge(high_ready, b.done)
                if b.later:
                    act.wait_ge(m1_ready, b.before)
                a.activation(EB[:], HIGH[:], ACT.Exp, scale=-1.0).then_inc(eb_ready, 1)

            @step
            def one(b, dst, src, func, src_ready, dst_ready, dst_used, **more):
                act.wait_ge(src_ready, b.done)
                if b.later:
                    act.wait_ge(dst_used, b.before)
                a.activation(dst[:], src[:], func, **more).then_inc(dst_ready, 1)

            @step
            def cmix_relu(b, n):
                act.wait_ge(kk_psum[n], b.done)
                if b.later:
                    act.wait_ge(kk_ready[n], b.before)
                a.activation(KR[:, n, :], bank_kk[n][:], ACT.Relu).then_inc(kr_ready[n], 1)

            @step
            def cmix_square(b, n):
                act.wait_ge(kr_ready[n], b.done)
                if b.later:
                    act.wait_ge(kv_psum, b.before)
                a.activation(KK[:, n, :], KR[:, n, :], ACT.Square).then_inc(kk_ready[n], 1)

            def iteration(s0, s1, s2, s3):
                one(s3, SG, RL2, ACT.Exp, rl2_ready, sg_ready, kvs_ready)
                evacuate(s1, f1.bank_T[:], f1.yT_psum, f1.yT[:], f1.yT_ready, [f1.h_psum[H - 1]])
                exp_high(s2)
                exp_low(s2)
                ffn_y_bias(s1, f1)
                ffn_relu(s1, f1, 0)
                ffn_relu(s1, f1, 2)
                ffn_relu(s1, f1, 1)
                one(s2, ER, AR, ACT.Exp, ar_ready, er_ready, dn_ready, scale=-1.0)
                ffn_relu(s1, f1, 3)
                normed(s0, na, X0, XN, xn_ready, [xnT_psum, gram_psum])
                normed(s3, f2.norm, X3, f2.y, f2.y_ready, [f2.yT_psum])
                one(s2, LD, DN, ACT.Ln, dn_ready, ld_ready, rl_ready)
                evacuate(s3, f2.bank_T[:], f2.yT_psum, f2.yT[:], f2.yT_ready, [f2.h_psum[H - 1]])
                one(s2, RC, RL, ACT.Exp, rl_ready, rc_ready, rw_ready)
                evacuate(s0, bank_aG[:, 0:C], gram_psum, GRAM[:], gram_ready, [proj_psum])
                ffn_y_bias(s3, f2)
                evacuate(s0, bank_aT[:], xnT_psum, XNT[:], xnT_ready, [attn_psum])
                ffn_relu(s3, f2, 0)
                evacuate(s0, bank_aP[:, 0:C], proj_psum, PROJ[:], proj_ready, [attn_psum])
                ffn_relu(s3, f2, 1)
                ffn_relu(s3, f2, 2)
                normed(s2, ncm, U1, NC, nc_ready, [ncT_psum])
                ffn_relu(s3, f2, 3)
                evacuate_affine(s2, ncT_psum, bank_cT, XC, "ln2_g", "ln2_b", xc_ready, [xk2_ready, xr2_ready])
                normed(s1, nt, X2, N, n_ready, [nT_psum, u1_ready])
                cmix_relu(s2, 0)
                evacuate_affine(s1, nT_psum, bank_tT, XA, "ln1_g", "ln1_b", xa_ready, [xk_ready, xv_ready, xr_ready])
                cmix_square(s2, 0)
                cmix_relu(s2, 2)
                cmix_square(s2, 2)
                cmix_relu(s2, 1)
                one(s2, AR2, bank_r2, ACT.Abs, r2_psum, ar2_ready, er2_ready)
                cmix_square(s2, 1)
                one(s2, ER2, AR2, ACT.Exp, ar2_ready, er2_ready, ld2_ready, scale=-1.0)
                cmix_relu(s2, 3)
                one(s2, LD2, ER2, ACT.Ln, er2_ready, ld2_ready, rl2_ready, bias=ONE[:])
                normed(s0, f1.norm, X1, f1.y, f1.y_ready, [f1.yT_psum])
                cmix_square(s2, 3)
                one(s1, AR, bank_r, ACT.Abs, r_psum, ar_ready, er_ready)

            a.preload_act_table_set("natural_log_exp_and_others")
            act.wait_ge(loaded["first"], 32)
            a.activation(WEXP[:], vec("decay"), ACT.Exp).then_inc(decay_exp, 1)
            act.wait_ge(decay_exp, 1)
            a.mul(WDEC[:], WEXP[:], -1.0).then_inc(decay_ready, 1)
            act.wait_ge(const_ready, 5)
            act.wait_ge(pads_ready, 4)
            act.wait_ge(loaded["ffn"], 80)
            each_iteration(act, iteration)

        @block.tensor
        def _(pe):
            t_ = nc.tensor

            def transposed(src, bank, done):
                for j in range(J):
                    last = t_.transpose(bank[:, j * P:(j + 1) * P], src[:, j, :], IDENT[:])
                last.then_inc(done, 1)

            @step
            def attn_transpose(b, users):
                pe.wait_ge(xn_ready, b.done)
                for s, count in b.freed(users):
                    pe.wait_ge(s, count)
                transposed(XN, bank_aT, xnT_psum)

            @step
            def attn_gram(b, users):
                pe.wait_ge(xn_ready, b.done)
                for s, count in b.freed(users):
                    pe.wait_ge(s, count)
                for j in range(J):
                    last = t_.matmul(bank_aG[:, 0:C], XN[:, j, :], XN[:, j, :], start=(j == 0), stop=(j == J - 1))
                last.then_inc(gram_psum, 1)

            @step
            def attn_proj(b, users):
                pe.wait_ge(gram_ready, b.done)
                for s, count in b.freed(users):
                    pe.wait_ge(s, count)
                t_.matmul(bank_aP[:, 0:C], Wq[:], GRAM[:], start=True, stop=True).then_inc(proj_psum, 1)

            @step
            def attn_apply(b, users):
                pe.wait_ge(proj_ready, b.done)
                pe.wait_ge(xnT_ready, b.done)
                for s, count in b.freed(users):
                    pe.wait_ge(s, count)
                for j in range(J):
                    last = t_.matmul(bank_aA[:, j * C:(j + 1) * C], XNT[:, j * P:(j + 1) * P], PROJ[:], start=True, stop=True)
                last.then_inc(attn_psum, 1)

            @step
            def ffn_transpose(b, f, users):
                pe.wait_ge(f.y_ready, b.done)
                for s, count in b.freed(users):
                    pe.wait_ge(s, count)
                transposed(f.y, f.bank_T, f.yT_psum)

            @step
            def ffn_hidden(b, f, n, users):
                pe.wait_ge(f.yT_ready, b.done)
                for s, count in b.freed(users):
                    pe.wait_ge(s, count)
                t_.matmul(f.bank_h[n][:], W1[:, n * P:(n + 1) * P], f.yT[:], start=True, stop=True).then_inc(f.h_psum[n], 1)

            @step
            def ffn_start(b, f, users):
                pe.wait_ge(f.yTb_ready, b.done)
                for s, count in b.freed(users):
                    pe.wait_ge(s, count)
                for j in range(J):
                    t_.matmul(f.bank_z[:, j * C:(j + 1) * C], f.yTb[:, j * P:(j + 1) * P], IDENT[:], start=(j == 0), stop=False,
                              is_transpose=True, skip_group_check=True)

            @step
            def ffn_down(b, f, n):
                pe.wait_ge(f.h_ready[n], b.done)
                for j in range(J):
                    last = t_.matmul(f.bank_z[:, j * C:(j + 1) * C], f.h[:, n, j * P:(j + 1) * P], W2[:, n, :], start=False,
                                     stop=(n == H - 1), skip_group_check=True)
                if n == H - 1:
                    last.then_inc(f.z_psum, 1)

            @step
            def tmix_transpose(b, users):
                pe.wait_ge(n_ready, b.done)
                for s, count in b.freed(users):
                    pe.wait_ge(s, count)
                transposed(N, bank_tT, nT_psum)

            @step
            def tmix_product(b, x, x_ready, w, bank, done, users):
                pe.wait_ge(x_ready, b.done)
                for s, count in b.freed(users):
                    pe.wait_ge(s, count)
                t_.matmul(bank[:], w[:], x[:], start=True, stop=True).then_inc(done, 1)

            @step
            def tmix_o(b, users):
                pe.wait_ge(rw_ready, b.done)
                for s, count in b.freed(users):
                    pe.wait_ge(s, count)
                for j in range(J):
                    last = t_.matmul(bank_o[:, j * C:(j + 1) * C], RW[:, j * P:(j + 1) * P], Wo[:], start=True, stop=True)
                last.then_inc(o_psum, 1)

            @step
            def cmix_transpose(b, users):
                pe.wait_ge(nc_ready, b.done)
                for s, count in b.freed(users):
                    pe.wait_ge(s, count)
                transposed(NC, bank_cT, ncT_psum)

            @step
            def cmix_up(b, n, users):
                pe.wait_ge(xk2_ready, b.done)
                for s, count in b.freed(users):
                    pe.wait_ge(s, count)
                t_.matmul(bank_kk[n][:], FWk[:, n * P:(n + 1) * P], XK2[:], start=True, stop=True).then_inc(kk_psum[n], 1)

            @step
            def cmix_down(b, n, users=()):
                pe.wait_ge(kk_ready[n], b.done)
                for s, count in b.freed(users):
                    pe.wait_ge(s, count)
                for j in range(J):
                    last = t_.matmul(bank_kv[:, j * C:(j + 1) * C], KK[:, n, j * P:(j + 1) * P], FWv[:, n, :],
                                     start=(n == 0 and j == 0), stop=(n == H - 1), skip_group_check=True)
                if n == H - 1:
                    last.then_inc(kv_psum, 1)

            @step
            def cmix_r(b, users):
                pe.wait_ge(xr2_ready, b.done)
                for s, count in b.freed(users):
                    pe.wait_ge(s, count)
                for j in range(J):
                    last = t_.matmul(bank_r2[:, j * C:(j + 1) * C], XR2[:, j * P:(j + 1) * P], FWr[:], start=True, stop=True)
                last.then_inc(r2_psum, 1)

            def iteration(s0, s1, s2, s3):
                ffn_hidden(s1, f1, 0,
                           [(kr_ready[3], s2.before), (x1_ready, s0.before), (f2.h_ready[1], s3.before), (f1.h_ready[0], s1.before)])
                ffn_hidden(s1, f1, 2,
                           [(rl2_ready, s2.before), (xa_ready, s1.before), (xc_ready, s2.before), (f2.h_ready[2], s3.before), (f1.h_ready[2], s1.before)])
                ffn_hidden(s1, f1, 1,
                           [(kr_ready[1], s2.before), (f2.yTb_ready, s3.before), (f1.h_ready[1], s1.before)])
                ffn_hidden(s1, f1, 3,
                           [(diff_ready, s1.before), (kr_ready[0], s2.before), (f2.h_ready[3], s3.before), (proj_ready, s0.before), (f1.h_ready[3], s1.before)])
                ffn_start(s1, f1, [(f1.yTb_ready, s0.before), (f2.zg_ready, s3.before), (f1.zg_ready, s1.before)])
                ffn_down(s1, f1, 0)
                ffn_down(s1, f1, 1)
                ffn_down(s1, f1, 2)
                ffn_down(s1, f1, 3)
                ffn_transpose(s3, f2, [(f1.h_ready[1], s1.done), (kr_ready[1], s2.before), (f2.yTb_ready, s3.before)])
                attn_gram(s0,
                          [(m2_ready, s1.before), (kr_ready[2], s2.before), (u1_ready, s2.before), (gram_ready, s0.before)])
                attn_transpose(s0, [(rl_ready, s1.before), (f2.h_ready[0], s3.before), (xnT_ready, s0.before)])
                ffn_hidden(s3, f2, 1,
                           [(f1.h_ready[0], s1.done), (kr_ready[3], s2.before), (x1_ready, s0.before), (f2.h_ready[1], s3.before)])
                tmix_o(s2,
                       [(gram_ready, s0.done), (m2_ready, s1.before), (kr_ready[2], s2.before), (u1_ready, s2.before)])
                ffn_hidden(s3, f2, 0, [(xnT_ready, s0.done), (rl_ready, s1.before), (f2.h_ready[0], s3.before)])
                attn_proj(s0,
                          [(f1.h_ready[3], s1.done), (diff_ready, s1.before), (kr_ready[0], s2.before), (f2.h_ready[3], s3.before), (proj_ready, s0.before)])
                ffn_start(s3, f2, [(f1.zg_ready, s1.done), (f1.yTb_ready, s0.before), (f2.zg_ready, s3.before)])
                ffn_hidden(s3, f2, 2,
                           [(f1.h_ready[2], s1.done), (rl2_ready, s2.before), (xa_ready, s1.before), (xc_ready, s2.before), (f2.h_ready[2], s3.before)])
                attn_apply(s0,
                           [(f2.h_ready[1], s3.done), (f1.h_ready[0], s1.done), (kr_ready[3], s2.before), (x1_ready, s0.before)])
                ffn_hidden(s3, f2, 3,
                           [(proj_ready, s0.done), (f1.h_ready[3], s1.done), (diff_ready, s1.before), (kr_ready[0], s2.before), (f2.h_ready[3], s3.before)])
                ffn_down(s3, f2, 0)
                ffn_down(s3, f2, 1)
                cmix_transpose(s2,
                               [(f2.h_ready[2], s3.done), (f1.h_ready[2], s1.done), (rl2_ready, s2.before), (xa_ready, s1.before), (xc_ready, s2.before)])
                ffn_down(s3, f2, 2)
                ffn_down(s3, f2, 3)
                cmix_up(s2, 0,
                        [(f2.h_ready[3], s3.done), (proj_ready, s0.done), (f1.h_ready[3], s1.done), (diff_ready, s1.before), (kr_ready[0], s2.before)])
                tmix_transpose(s1,
                               [(xc_ready, s2.done), (f2.h_ready[2], s3.done), (f1.h_ready[2], s1.done), (rl2_ready, s2.before), (xa_ready, s1.before)])
                cmix_up(s2, 2,
                        [(u1_ready, s2.done), (gram_ready, s0.done), (m2_ready, s1.before), (kr_ready[2], s2.before)])
                cmix_up(s2, 1, [(f2.yTb_ready, s3.done), (f1.h_ready[1], s1.done), (kr_ready[1], s2.before)])
                cmix_r(s2,
                       [(xa_ready, s1.done), (xc_ready, s2.done), (f2.h_ready[2], s3.done), (f1.h_ready[2], s1.done), (rl2_ready, s2.before)])
                cmix_up(s2, 3,
                        [(x1_ready, s0.done), (f2.h_ready[1], s3.done), (f1.h_ready[0], s1.done), (kr_ready[3], s2.before)])
                tmix_product(s1, XK, xk_ready, Wk, bank_k, k_psum,
                             [(kr_ready[0], s2.done), (f2.h_ready[3], s3.done), (proj_ready, s0.done), (f1.h_ready[3], s1.done), (diff_ready, s1.before)])
                cmix_down(s2, 0, [(kvs_ready, s2.before)])
                tmix_product(s1, XR, xr_ready, Wr, bank_r, r_psum,
                             [(f2.h_ready[0], s3.done), (xnT_ready, s0.done), (rl_ready, s1.before)])
                cmix_down(s2, 1)
                cmix_down(s2, 2)
                ffn_transpose(s0, f1, [(f2.zg_ready, s3.done), (f1.zg_ready, s1.done), (f1.yTb_ready, s0.before)])
                cmix_down(s2, 3)
                tmix_product(s1, XV, xv_ready, Wv, bank_v, v_psum,
                             [(kr_ready[2], s2.done), (u1_ready, s2.done), (gram_ready, s0.done), (m2_ready, s1.before)])

            pe.wait_ge(ident_ready, 1)
            pe.wait_ge(loaded["first"], 32)
            pe.wait_ge(loaded["ffn"], 80)
            pe.wait_ge(loaded["tmix"], 64)
            pe.wait_ge(loaded["cmix"], 48)
            each_iteration(pe, iteration)


def kernel(**inputs):
    import numpy as np
    import concourse.bacc as bacc
    from concourse.bass_utils import run_bass_kernel_spmd

    get = {n: np.asarray(a) for n, a in inputs.items()}
    rw = {n[len("L0_attn_b_"):]: a for n, a in get.items() if n.startswith("L0_attn_b_")}
    ffn = {n[len("L0_ffn_"):]: a for n, a in get.items() if n.startswith("L0_ffn_")}
    hidden = get["L0_attn_a_hidden_states"]
    C = hidden.shape[2]
    J = hidden.shape[1] // P
    vectors = {"ln1_g": rw["ln1_g"], "ln1_b": rw["ln1_b"], "ln2_g": rw["ln2_g"], "ln2_b": rw["ln2_b"],
               "decay": rw["time_decay"], "first": rw["time_first"], "mix_k": rw["time_mix_k"],
               "mix_v": rw["time_mix_v"], "mix_r": rw["time_mix_r"], "cm_k": rw["cm_k"], "cm_r": rw["cm_r"],
               "b2": ffn["b2"][0]}
    laid = {
        "hidden": hidden, "w_q": get["L0_attn_a_W_q"],
        "w1": ffn["w1"][0], "w2": ffn["w2"][0], "b1": ffn["b1"][0].reshape(-1, P).T,
        "wk": rw["att_Wk"].T, "wv": rw["att_Wv"].T, "wr": rw["att_Wr"].T, "wo": rw["att_Wo"].T,
        "f_wk": rw["ffn_Wk"].T, "f_wr": rw["ffn_Wr"].T, "f_wv": rw["ffn_Wv"].T,
        "vectors": np.stack([vectors[n] for n in VECTORS], axis=1),
        "gamma": np.tile(ffn["gamma"], (P, 1)), "beta": np.tile(ffn["beta"], (P, J)),
    }
    nc = bacc.Bacc("TRN2", target_bir_lowering=False, num_devices=1)
    arrays, args = {}, []
    for name, a in laid.items():
        a = np.ascontiguousarray(a)
        arrays["in_" + name] = a
        args.append(nc.dram_tensor("in_" + name, a.shape, mybir.dt.from_np(a.dtype), kind="ExternalInput").ap())
    args.append(nc.dram_tensor("out_x", hidden.shape, F32, kind="ExternalOutput").ap())
    hybrid_layer(nc, *args)
    return run_bass_kernel_spmd(nc, [arrays], core_ids=[0]).results[0]["out_x"]
```

```python
from contextlib import ExitStack

import concourse.bass as bass
from concourse import mybir
from concourse.alu_op_type import AluOpType as ALU

F32 = mybir.dt.float32
ACT = mybir.ActivationFunctionType

P = 128
EPS = 1e-5
MIN_LOG = -1e38
STAGES = 4
QUIET_UNTIL = 2
WARM_UP = 16
DMA = 16

VECTORS = ["ln1_g", "ln1_b", "ln2_g", "ln2_b", "decay", "first", "mix_k", "mix_v", "mix_r", "cm_k", "cm_r", "b2"]


class At:

    def __init__(self, values, offset, active=True, quiet=False):
        self.values, self.offset, self.active, self.quiet = values, offset, active, quiet
        self.done, self.before = values[1][offset + 1], values[1][offset]
        self.looped = not isinstance(self.before, int)
        self.later = self.looped or self.before > 0
        self.first = not self.later

    def count(self, more=0, each=1):
        return self.values[each][self.offset + more]

    def freed(self, users):
        return users[:1] if self.looped else [(s, n) for s, n in users if n > 0]


def step(program):
    def run(b, *args, **more):
        if b.active:
            program(b, *args, **more)
    return run


def hybrid_layer(nc, hidden, w_q, w1, w2, b1, wk, wv, wr, wo, f_wk, f_wr, f_wv, vectors, gamma, beta, out):
    B, T, C = hidden.shape
    J = T // P
    H = w1.shape[1] // P
    assert C == P and f_wk.shape[1] == H * P

    with ExitStack() as ctx:
        def sb(name, shape):
            return ctx.enter_context(nc.sbuf_tensor(name, shape, F32))

        def sem(name):
            return ctx.enter_context(nc.semaphore(name))

        def rows(name):
            return sb(name, [P, J, P])

        def cols(name):
            return sb(name, [P, T])

        Wq = sb("Wq", [P, C])
        W1 = sb("W1", [P, H * P])
        W2 = sb("W2", [P, H, C])
        Wk, Wv, Wr, Wo, FWr = (sb(n, [P, C]) for n in ("Wk", "Wv", "Wr", "Wo", "FWr"))
        FWk = sb("FWk", [P, H * P])
        FWv = sb("FWv", [P, H, C])
        B1 = sb("B1", [P, H])
        VEC = sb("VEC", [P, len(VECTORS)])
        GAMMA = sb("GAMMA", [P, C])
        BETA = sb("BETA", [P, J, C])
        IDENT = sb("IDENT", [P, P])
        ONE = sb("ONE", [P, 1])
        WDEC = sb("WDEC", [P, 1])
        WEXP = sb("WEXP", [P, 1])
        WROW = sb("WROW", [P, T])
        K_EPS, K_NEG, K_RSQRT = (sb(n, [P, 2 * J]) for n in ("K_EPS", "K_NEG", "K_RSQRT"))

        def vec(name):
            n = VECTORS.index(name)
            return VEC[:, n:n + 1]

        banks = [ctx.enter_context(nc.psum_tensor(f"bank{n}", [P, T], F32)) for n in range(8)]
        bank_aT, bank_aG, bank_aP, bank_aA = banks[4], banks[3], banks[5], banks[5]
        bank_tT, bank_k, bank_v, bank_r, bank_o = banks[2], banks[0], banks[2], banks[5], banks[7]
        bank_cT, bank_r2, bank_kv = banks[7], banks[1], banks[3]
        bank_kk = [banks[5], banks[0], banks[6], banks[7]]
        f1_banks = {"T": banks[6], "h": [banks[4], banks[0], banks[4], banks[2]], "z": banks[6]}
        f2_banks = {"T": banks[0], "h": [banks[4], banks[2], banks[1], banks[0]], "z": banks[4]}
        loaded = {n: sem("loaded_" + n) for n in ("first", "ffn", "tmix", "cmix")}
        const_ready = sem("const_ready")
        ident_ready = sem("ident_ready")
        decay_exp, decay_ready, decay_row = sem("decay_exp"), sem("decay_ready"), sem("decay_row")
        pads_ready = sem("pads_ready")

        class Norm:

            def __init__(self, n, kind="plain"):
                self.stats = sb(n + "_stats", [P, J, 6])
                self.mv = sb(n + "_mv", [P, J, 2])
                self.ve = sb(n + "_ve", [P, 2 * J])
                self.tmp = sb(n + "_tmp", [P, J])
                self.carry = sb(n + "_carry", [P, 1])
                self.nm = sb(n + "_nm", [P, J])
                self.rs = sb(n + "_rs", [P, 2 * J])
                self.nb = sb(n + "_nb", [P, J])
                self.back = sb(n + "_back", [P, J])
                self.stats_done = sem(n + "_stats_done")
                self.mv_ready = sem(n + "_mv_ready")
                self.ve_ready = sem(n + "_ve_ready")
                self.rs_ready = sem(n + "_rs_ready")
                if kind != "scale only":
                    self.nb_ready = sem(n + "_nb_ready")
                if kind == "twice":
                    self.tmp_ready = sem(n + "_tmp_ready")
                    self.q_ready = sem(n + "_q_ready")

        class Ffn:

            def __init__(self, n, x, x_ready, y_out, out_used, banks):
                self.bank_T, self.bank_h, self.bank_z = banks["T"], banks["h"], banks["z"]
                self.z_rows = self.bank_z[:].rearrange("p (j c) -> p j c", j=J)
                self.x, self.x_ready = x, x_ready
                self.norm, self.znorm = Norm(n + "_y"), Norm(n + "_z", "scale only")
                self.xb, self.xb_ready = rows(n + "_xb"), sem(n + "_xb_ready")
                self.y, self.y_ready = rows(n + "_y"), sem(n + "_y_ready")
                self.yT_psum, self.yT_ready = sem(n + "_yT_psum"), sem(n + "_yT_ready")
                self.yT = cols(n + "_yT")
                self.yTb, self.yTb_ready = cols(n + "_yTb"), sem(n + "_yTb_ready")
                self.h = sb(n + "_h", [P, H, T])
                self.h_psum = [sem(f"{n}_h{f}_psum") for f in range(H)]
                self.h_ready = [sem(f"{n}_h{f}_ready") for f in range(H)]
                self.z_psum = sem(n + "_z_psum")
                self.zg, self.zg_ready = rows(n + "_zg"), sem(n + "_zg_ready")
                self.out, self.out_ready = y_out, sem(n + "_out_ready")
                self.out_used = out_used

        X0, x0_loaded = rows("X0"), sem("x0_loaded")
        na = Norm("attn")
        XN, xn_ready = rows("XN"), sem("xn_ready")
        xnT_psum, xnT_ready = sem("xnT_psum"), sem("xnT_ready")
        XNT = cols("XNT")
        GRAM, gram_psum, gram_ready = sb("GRAM", [P, C]), sem("gram_psum"), sem("gram_ready")
        PROJ, proj_psum, proj_ready = sb("PROJ", [P, C]), sem("proj_psum"), sem("proj_ready")
        attn_psum = sem("attn_psum")
        X1, x1_ready = rows("X1"), sem("x1_ready")
        X2, X3, X4 = rows("X2"), rows("X3"), rows("X4")

        x2_kept = sem("x2_kept")
        stored = sem("stored")
        nt = Norm("tmix", "twice")
        X2K = rows("X2K")
        back_half, back_ready = sem("back_half"), sem("back_ready")
        N, n_ready = rows("N"), sem("n_ready")
        nT_psum = sem("nT_psum")
        XA, xa_ready = sb("XA", [P, T + 1]), sem("xa_ready")
        DX, dx_ready = cols("DX"), sem("dx_ready")
        XK, xk_ready = cols("XK"), sem("xk_ready")
        XV, xv_ready = cols("XV"), sem("xv_ready")
        XR, xr_ready = cols("XR"), sem("xr_ready")
        k_psum, v_psum, r_psum = sem("k_psum"), sem("v_psum"), sem("r_psum")
        PP, pp_ready = sb("PP", [P, T + 1]), sem("pp_ready")
        DIFF, diff_ready = sb("DIFF", [P, 2, T]), sem("diff_ready")
        LOW, low_ready = sb("LOW", [P, 2, T]), sem("low_ready")
        HIGH, high_ready = sb("HIGH", [P, 2, T]), sem("high_ready")
        EA, ea_ready = sb("EA", [P, 3, T]), sem("ea_ready")
        EB, eb_ready = sb("EB", [P, 2, T]), sem("eb_ready")
        EV, ev_ready = cols("EV"), sem("ev_ready")
        AB, ab_ready, b_ready = sb("AB", [P, 2, T + 1]), sem("ab_ready"), sem("b_ready")
        m2_ready = sem("m2_ready")
        M1, m1_ready = sb("M1", [P, 2, T]), sem("m1_ready")
        ND, nd_ready = sb("ND", [P, 2, T]), sem("nd_ready")
        AR, ar_ready = cols("AR"), sem("ar_ready")
        ER, er_ready = cols("ER"), sem("er_ready")
        DN, dn_ready = cols("DN"), sem("dn_ready")
        LD, ld_ready = cols("LD"), sem("ld_ready")
        RL, rl_ready = cols("RL"), sem("rl_ready")
        RC, rc_ready = cols("RC"), sem("rc_ready")
        RW, rw_ready = cols("RW"), sem("rw_ready")
        o_psum = sem("o_psum")
        U1, u1_ready = rows("U1"), sem("u1_ready")
        X2U, x2u_ready = rows("X2U"), sem("x2u_ready")

        ncm = Norm("cmix")
        NC, nc_ready = rows("NC"), sem("nc_ready")
        ncT_psum = sem("ncT_psum")
        XC, xc_ready = sb("XC", [P, T + 1]), sem("xc_ready")
        DC, dc_ready = cols("DC"), sem("dc_ready")
        XK2, xk2_ready = cols("XK2"), sem("xk2_ready")
        XR2, xr2_ready = cols("XR2"), sem("xr2_ready")
        kk_psum = [sem(f"kk{f}_psum") for f in range(H)]
        KR, kr_ready = sb("KR", [P, H, T]), [sem(f"kr{f}_ready") for f in range(H)]
        KK, kk_ready = sb("KK", [P, H, T]), [sem(f"kk{f}_ready") for f in range(H)]
        kv_psum, r2_psum = sem("kv_psum"), sem("r2_psum")
        AR2, ar2_ready = cols("AR2"), sem("ar2_ready")
        ER2, er2_ready = cols("ER2"), sem("er2_ready")
        LD2, ld2_ready = cols("LD2"), sem("ld2_ready")
        RL2, rl2_ready = cols("RL2"), sem("rl2_ready")
        SG, sg_ready = cols("SG"), sem("sg_ready")
        KVS, kvs_ready = cols("KVS"), sem("kvs_ready")
        x3_ready = sem("x3_ready")

        f1 = Ffn("f1", X1, x1_ready, X2, [(x2_kept, DMA), (n_ready, 1)], f1_banks)
        f2 = Ffn("f2", X3, x3_ready, X4, [(stored, DMA)], f2_banks)
        x2_ready, x4_ready = f1.out_ready, f2.out_ready

        def each_iteration(engines, body, after_first=None, dma_counts=()):
            first, last = STAGES, B
            stages = lambda values, i: [
                At(values, -s, i is None or 0 <= i - s < B, i is not None and not QUIET_UNTIL <= i < B + STAGES - 1 - QUIET_UNTIL)
                for s in range(STAGES)]
            span = range(-STAGES, 2)

            def numbers(i):
                return {each: {k: max(0, min(i + k, B)) * each for k in span} for each in (1, DMA)}

            for i in range(first):
                body(*stages(numbers(i), i))
                if i == 0 and after_first is not None:
                    after_first()
            with engines.Fori(first, last) as i:
                def held(value, name):
                    register = engines.alloc_register(name)
                    engines.reg_mov(register, value)
                    return engines.snap(register)

                registers = {1: {k: held(i + k, f"n{k + STAGES}") for k in range(-STAGES + 1, 2)}}
                registers[DMA] = {k: held((i + k) * DMA, f"dma{k + STAGES}") for k in dma_counts}
                body(*stages(registers, None))
            for i in range(last, B + STAGES - 1):
                body(*stages(numbers(i), i))

        block = ctx.enter_context(nc.Block())

        @block.sync
        def _(sp):
            x0_dram = hidden.rearrange("b t c -> (b t) c")
            out_dram = out.rearrange("b t c -> (b t) c")

            @step
            def load_x0(b):
                if b.later:
                    sp.wait_ge(x1_ready, b.before)
                sp.dma_start(X0[:], of(x0_dram, b)).then_inc(x0_loaded, DMA)

            @step
            def keep_x2(b):
                sp.wait_ge(x2_ready, b.done)
                if b.later:
                    sp.wait_ge(x2u_ready, b.before)
                sp.dma_start(X2K[:], X2[:]).then_inc(x2_kept, DMA)

            @step
            def store(b):
                sp.wait_ge(x4_ready, b.done)
                sp.dma_start(of(out_dram, b), X4[:]).then_inc(stored, DMA)

            def of(dram, b):
                return dram[bass.ds(b.count() * T, T), :].rearrange("(j p) c -> p j c", p=P)

            def iteration(s0, s1, s2, s3):
                load_x0(s0)
                keep_x2(s2)
                store(s3)

            def weights():
                sp.dma_start(Wq[:], w_q).then_inc(loaded["first"], 16)
                sp.dma_start(VEC[:], vectors).then_inc(loaded["first"], 16)
                sp.dma_start(W1[:], w1).then_inc(loaded["ffn"], 16)
                sp.dma_start(B1[:], b1).then_inc(loaded["ffn"], 16)
                sp.dma_start(W2[:], w2.rearrange("(f p) c -> p f c", p=P)).then_inc(loaded["ffn"], 16)
                sp.dma_start(GAMMA[:], gamma).then_inc(loaded["ffn"], 16)
                sp.dma_start(BETA[:].rearrange("p j c -> p (j c)"), beta).then_inc(loaded["ffn"], 16)
                for t, d in ((Wk, wk), (Wv, wv), (Wr, wr), (Wo, wo)):
                    sp.dma_start(t[:], d).then_inc(loaded["tmix"], 16)
                sp.dma_start(FWk[:], f_wk).then_inc(loaded["cmix"], 16)
                sp.dma_start(FWr[:], f_wr).then_inc(loaded["cmix"], 16)
                sp.dma_start(FWv[:], f_wv.rearrange("(f p) c -> p f c", p=P)).then_inc(loaded["cmix"], 16)

            each_iteration(sp, iteration, after_first=weights)
            sp.wait_ge(stored, DMA * B)

        @block.gpsimd
        def _(pool):
            pool.memset(K_EPS[:], EPS).then_inc(const_ready, 1)
            pool.memset(K_NEG[:], -1.0).then_inc(const_ready, 1)
            pool.memset(K_RSQRT[:], -0.5).then_inc(const_ready, 1)
            pool.memset(ONE[:], 1.0).then_inc(const_ready, 1)
            pool.memset(IDENT[:], 0.0).then_inc(const_ready, 1)
            pool.wait_ge(const_ready, 5)
            pool.affine_select(out=IDENT[:], in_=IDENT[:], compare_op=ALU.not_equal, fill=1.0, base=0,
                               pattern=[[-1, P]], channel_multiplier=1).then_inc(ident_ready, 1)
            pool.memset(XA[:, 0:1], 0.0).then_inc(pads_ready, 1)
            pool.memset(XC[:, 0:1], 0.0).then_inc(pads_ready, 1)
            pool.memset(AB[:, :, 0:1], 0.0).then_inc(pads_ready, 1)
            pool.memset(PP[:, 0:1], MIN_LOG).then_inc(pads_ready, 1)

            @step
            def scale(b, n, users, with_bias=True):
                pool.wait_ge(n.mv_ready, b.done)
                for s in users:
                    if b.later:
                        pool.wait_ge(s, b.before)
                pool.tensor_tensor(n.ve[:, 0:J], n.mv[:, :, 1], K_EPS[:, 0:J], ALU.add).then_inc(n.ve_ready, 1)
                if with_bias:
                    pool.tensor_tensor(n.nm[:], n.mv[:, :, 0], K_NEG[:, 0:J], ALU.mult)
                pool.wait_ge(n.ve_ready, b.done)
                pool.tensor_tensor(n.rs[:, 0:J], n.ve[:, 0:J], K_RSQRT[:, 0:J], ALU.pow).then_inc(n.rs_ready, 1)
                if with_bias:
                    pool.wait_ge(n.rs_ready, b.done)
                    pool.tensor_tensor(n.nb[:], n.nm[:], n.rs[:, 0:J], ALU.mult).then_inc(n.nb_ready, 1)

            @step
            def scale_twice(b, n):
                pool.wait_ge(n.mv_ready, b.done)
                if b.later:
                    pool.wait_ge(back_ready, b.before)
                if b.later:
                    pool.wait_ge(n_ready, b.before)
                pool.tensor_tensor(n.ve[:, J:], n.mv[:, :, 1], K_EPS[:, 0:J], ALU.add).then_inc(n.ve_ready, 1)
                pool.tensor_tensor(n.nm[:], n.mv[:, :, 0], K_NEG[:, 0:J], ALU.mult)
                pool.wait_ge(n.ve_ready, b.done)
                pool.tensor_tensor(n.tmp[:], n.ve[:, J:], K_EPS[:, 0:J], ALU.mult).then_inc(n.tmp_ready, 1)
                pool.wait_ge(n.tmp_ready, b.done)
                pool.tensor_tensor(n.ve[:, 0:J], n.mv[:, :, 1], n.tmp[:], ALU.add).then_inc(n.q_ready, 1)
                pool.wait_ge(n.q_ready, b.done)
                pool.tensor_tensor(n.rs[:], n.ve[:], K_RSQRT[:], ALU.pow).then_inc(n.rs_ready, 1)
                pool.wait_ge(n.rs_ready, b.done)
                pool.tensor_tensor(n.nb[:], n.nm[:], n.rs[:, 0:J], ALU.mult).then_inc(n.nb_ready, 1)

            @step
            def back_scale(b, n):
                pool.wait_ge(n.rs_ready, b.done)
                if b.later:
                    pool.wait_ge(u1_ready, b.before)
                pool.tensor_tensor(n.tmp[:], n.ve[:, 0:J], n.rs[:, 0:J], ALU.mult).then_inc(back_half, 1)
                pool.wait_ge(back_half, b.done)
                pool.tensor_tensor(n.back[:], n.tmp[:], n.rs[:, J:], ALU.mult).then_inc(back_ready, 1)

            def iteration(s0, s1, s2, s3):
                scale(s0, na, [xn_ready])
                scale(s1, f1.znorm, [f1.out_ready], with_bias=False)
                scale(s2, ncm, [nc_ready])
                scale_twice(s1, nt)
                scale(s3, f2.znorm, [f2.out_ready], with_bias=False)
                back_scale(s1, nt)
                scale(s0, f1.norm, [f1.y_ready])
                scale(s2, f2.norm, [f2.y_ready])

            each_iteration(pool, iteration)

        @block.vector
        def _(dve):
            v = nc.vector

            @step
            def stats(b, n, src, src_ready, each=1):
                dve.wait_ge(src_ready, b.count(1, each))
                if b.later:
                    dve.wait_ge(n.mv_ready, b.before)
                for j in range(J):
                    last = v.bn_stats(n.stats[:, j, :], src[:, j, :])
                last.then_inc(n.stats_done, 1)

            @step
            def mean_var(b, n, scale_ready):
                if b.later:
                    dve.wait_ge(scale_ready, b.before)
                dve.wait_ge(n.stats_done, b.done)
                v.memset(n.carry[:], 0.0)
                for j in range(J):
                    last = v.bn_aggr(n.mv[:, j, :], n.stats[:, j, :])
                last.then_inc(n.mv_ready, 1)

            @step
            def attn_out(b):
                dve.wait_ge(attn_psum, b.done)
                if b.later:
                    dve.wait_ge(f1.y_ready, b.before)
                if b.later:
                    dve.wait_ge(f1.xb_ready, b.before)
                v.tensor_tensor(X1[:], bank_aA[:].rearrange("p (j c) -> p j c", j=J), X0[:], ALU.add).then_inc(x1_ready, 1)

            @step
            def ffn_residual(b, f):
                if b.first:
                    dve.wait_ge(loaded["ffn"], 5 * DMA)
                dve.wait_ge(f.x_ready, b.done)
                if b.later:
                    dve.wait_ge(f.out_ready, b.before)
                v.tensor_tensor(f.xb[:], f.x[:], BETA[:], ALU.add).then_inc(f.xb_ready, 1)

            @step
            def ffn_gain(b, f):
                if b.first:
                    dve.wait_ge(loaded["ffn"], 5 * DMA)
                dve.wait_ge(f.znorm.mv_ready, b.done)
                if b.later:
                    dve.wait_ge(f.out_ready, b.before)
                for j in range(J):
                    last = v.scalar_tensor_tensor(f.zg[:, j, :], f.z_rows[:, j, :], f.znorm.mv[:, j, 0:1], GAMMA[:],
                                                  ALU.subtract, ALU.mult)
                last.then_inc(f.zg_ready, 1)

            @step
            def ffn_out(b, f):
                dve.wait_ge(f.znorm.rs_ready, b.done)
                dve.wait_ge(f.zg_ready, b.done)
                dve.wait_ge(f.xb_ready, b.done)
                for s, each in f.out_used:
                    if b.later:
                        dve.wait_ge(s, b.count(0, each))
                for j in range(J):
                    last = v.scalar_tensor_tensor(f.out[:, j, :], f.zg[:, j, :], f.znorm.rs[:, j:j + 1], f.xb[:, j, :],
                                                  ALU.mult, ALU.add)
                last.then_inc(f.out_ready, 1)

            @step
            def change(b, x, x_ready, diff, diff_ready, diff_used):
                dve.wait_ge(x_ready, b.done)
                for s in diff_used:
                    if b.later:
                        dve.wait_ge(s, b.before)
                v.tensor_tensor(diff[:], x[:, 1:], x[:, 0:T], ALU.subtract).then_inc(diff_ready, 1)

            @step
            def mix(b, x, diff, diff_ready, weight, dst, dst_ready, dst_used):
                dve.wait_ge(diff_ready, b.done)
                if b.later:
                    dve.wait_ge(dst_used, b.before)
                v.scalar_tensor_tensor(dst[:], diff[:], vec(weight), x[:, 0:T], ALU.mult, ALU.add).then_inc(dst_ready, 1)

            @step
            def running_max(b):
                dve.wait_ge(k_psum, b.done)
                if b.later:
                    dve.wait_ge(diff_ready, b.before)
                v.tensor_tensor_scan(PP[:, 1:], WROW[:], bank_k[:], MIN_LOG, ALU.add, ALU.max).then_inc(pp_ready, 1)

            @step
            def differences(b):
                dve.wait_ge(pp_ready, b.done)
                if b.later:
                    dve.wait_ge(low_ready, b.before)
                if b.later:
                    dve.wait_ge(high_ready, b.before)
                v.scalar_tensor_tensor(DIFF[:, 0, :], PP[:, 0:T], WDEC[:], bank_k[:], ALU.add, ALU.subtract)
                v.scalar_tensor_tensor(DIFF[:, 1, :], bank_k[:], vec("first"), PP[:, 0:T],
                                       ALU.add, ALU.subtract).then_inc(diff_ready, 1)

            @step
            def exponents_low(b):
                dve.wait_ge(diff_ready, b.done)
                if b.later:
                    dve.wait_ge(ea_ready, b.before)
                v.tensor_scalar(LOW[:], DIFF[:], 0.0, None, ALU.min).then_inc(low_ready, 1)

            @step
            def exponents_high(b):
                dve.wait_ge(diff_ready, b.done)
                if b.later:
                    dve.wait_ge(eb_ready, b.before)
                v.tensor_scalar(HIGH[:], DIFF[:], 0.0, None, ALU.max).then_inc(high_ready, 1)

            @step
            def new_values(b):
                dve.wait_ge(eb_ready, b.done)
                dve.wait_ge(v_psum, b.done)
                if b.later:
                    dve.wait_ge(ab_ready, b.before)
                v.tensor_tensor(EV[:], EB[:, 0, :], bank_v[:], ALU.mult).then_inc(ev_ready, 1)

            @step
            def first_values(b):
                dve.wait_ge(ea_ready, b.done)
                dve.wait_ge(v_psum, b.done)
                if b.later:
                    dve.wait_ge(nd_ready, b.before)
                v.tensor_tensor(EA[:, 1, :], EA[:, 2, :], bank_v[:], ALU.mult).then_inc(m2_ready, 1)

            @step
            def denominator_sum(b):
                dve.wait_ge(ea_ready, b.done)
                dve.wait_ge(eb_ready, b.done)
                if b.later:
                    dve.wait_ge(m1_ready, b.before)
                v.tensor_tensor_scan(AB[:, 1, 1:], EA[:, 0, :], EB[:, 0, :], 0.0, ALU.mult, ALU.add).then_inc(b_ready, 1)

            @step
            def numerator_sum(b):
                dve.wait_ge(ev_ready, b.done)
                dve.wait_ge(ea_ready, b.done)
                if b.later:
                    dve.wait_ge(m1_ready, b.before)
                v.tensor_tensor_scan(AB[:, 0, 1:], EA[:, 0, :], EV[:], 0.0, ALU.mult, ALU.add).then_inc(ab_ready, 1)

            @step
            def weighted(b):
                dve.wait_ge(b_ready, b.done)
                dve.wait_ge(ab_ready, b.done)
                if b.later:
                    dve.wait_ge(nd_ready, b.before)
                v.tensor_tensor(M1[:], AB[:, :, 0:T], EB[:, 1:2, :].broadcast_to([P, 2, T]), ALU.mult).then_inc(m1_ready, 1)

            @step
            def with_current(b):
                dve.wait_ge(m1_ready, b.done)
                dve.wait_ge(m2_ready, b.done)
                if b.later:
                    dve.wait_ge(rw_ready, b.before)
                if b.later:
                    dve.wait_ge(dn_ready, b.before)
                v.tensor_tensor(ND[:], M1[:], EA[:, 1:3, :], ALU.add).then_inc(nd_ready, 1)

            @step
            def gate_sum(b):
                dve.wait_ge(nd_ready, b.done)
                dve.wait_ge(er_ready, b.done)
                if b.later:
                    dve.wait_ge(ld_ready, b.before)
                v.scalar_tensor_tensor(DN[:], ER[:], 1.0, ND[:, 1, :], ALU.add, ALU.mult).then_inc(dn_ready, 1)

            @step
            def gate_log(b):
                dve.wait_ge(ld_ready, b.done)
                if b.later:
                    dve.wait_ge(rc_ready, b.before)
                v.scalar_tensor_tensor(RL[:], bank_r[:], 0.0, LD[:], ALU.min, ALU.subtract).then_inc(rl_ready, 1)

            @step
            def gated(b):
                dve.wait_ge(rc_ready, b.done)
                if b.later:
                    dve.wait_ge(o_psum, b.before)
                v.tensor_tensor(RW[:], ND[:, 0, :], RC[:], ALU.mult).then_inc(rw_ready, 1)

            @step
            def tmix_out(b):
                dve.wait_ge(o_psum, b.done)
                dve.wait_ge(back_ready, b.done)
                if b.later:
                    dve.wait_ge(nc_ready, b.before)
                if b.later:
                    dve.wait_ge(x2u_ready, b.before)
                o = bank_o[:].rearrange("p (j c) -> p j c", j=J)
                for j in range(J):
                    last = v.scalar_tensor_tensor(U1[:, j, :], N[:, j, :], nt.back[:, j:j + 1], o[:, j, :],
                                                  ALU.mult, ALU.add)
                last.then_inc(u1_ready, 1)

            @step
            def tmix_residual(b):
                dve.wait_ge(u1_ready, b.done)
                dve.wait_ge(x2_kept, b.count(1, DMA))
                if b.later:
                    dve.wait_ge(x3_ready, b.before)
                v.tensor_tensor(X2U[:], X2K[:], U1[:], ALU.add).then_inc(x2u_ready, 1)

            @step
            def cgate_log(b):
                dve.wait_ge(ld2_ready, b.done)
                if b.later:
                    dve.wait_ge(sg_ready, b.before)
                v.scalar_tensor_tensor(RL2[:], bank_r2[:], 0.0, LD2[:], ALU.min, ALU.subtract).then_inc(rl2_ready, 1)

            @step
            def cmix_gated(b):
                dve.wait_ge(sg_ready, b.done)
                dve.wait_ge(kv_psum, b.done)
                if b.later:
                    dve.wait_ge(x3_ready, b.before)
                v.tensor_tensor(KVS[:], bank_kv[:], SG[:], ALU.mult).then_inc(kvs_ready, 1)

            @step
            def cmix_out(b):
                dve.wait_ge(kvs_ready, b.done)
                dve.wait_ge(x2u_ready, b.done)
                if b.later:
                    dve.wait_ge(f2.y_ready, b.before)
                if b.later:
                    dve.wait_ge(f2.xb_ready, b.before)
                v.tensor_tensor(X3[:], KVS[:].rearrange("p (j c) -> p j c", j=J), X2U[:], ALU.add).then_inc(x3_ready, 1)

            def iteration(s0, s1, s2, s3):
                with_current(s2)
                gate_sum(s2)
                stats(s0, na, X0, x0_loaded, each=DMA)
                gate_log(s2)
                mean_var(s0, na, na.nb_ready)
                stats(s1, f1.znorm, f1.z_rows, f1.z_psum)
                gated(s2)
                mean_var(s1, f1.znorm, f1.znorm.rs_ready)
                ffn_gain(s1, f1)
                tmix_out(s2)
                stats(s2, ncm, U1, u1_ready)
                mean_var(s2, ncm, ncm.nb_ready)
                ffn_out(s1, f1)
                ffn_residual(s3, f2)
                stats(s1, nt, X2, x2_ready)
                mean_var(s1, nt, back_ready)
                attn_out(s0)
                tmix_residual(s2)
                stats(s0, f1.norm, X1, f1.x_ready)
                change(s2, XC, xc_ready, DC, dc_ready, [xk2_ready, xr2_ready])
                mix(s2, XC, DC, dc_ready, "cm_r", XR2, xr2_ready, r2_psum)
                mean_var(s0, f1.norm, f1.norm.nb_ready)
                mix(s2, XC, DC, dc_ready, "cm_k", XK2, xk2_ready, kk_psum[H - 1])
                stats(s3, f2.znorm, f2.z_rows, f2.z_psum)
                ffn_residual(s0, f1)
                mean_var(s3, f2.znorm, f2.znorm.rs_ready)
                change(s1, XA, xa_ready, DX, dx_ready, [xk_ready, xv_ready, xr_ready])
                ffn_gain(s3, f2)
                mix(s1, XA, DX, dx_ready, "mix_k", XK, xk_ready, k_psum)
                mix(s1, XA, DX, dx_ready, "mix_v", XV, xv_ready, v_psum)
                mix(s1, XA, DX, dx_ready, "mix_r", XR, xr_ready, r_psum)
                running_max(s1)
                cgate_log(s2)
                differences(s1)
                ffn_out(s3, f2)
                exponents_low(s1)
                cmix_gated(s2)
                exponents_high(s1)
                cmix_out(s2)
                stats(s2, f2.norm, X3, f2.x_ready)
                denominator_sum(s1)
                new_values(s1)
                mean_var(s2, f2.norm, f2.norm.nb_ready)
                numerator_sum(s1)
                first_values(s1)
                weighted(s1)

            def decay_along_tokens():
                dve.wait_ge(pads_ready, 4)
                dve.wait_ge(loaded["first"], 2 * DMA)
                dve.wait_ge(decay_ready, 1)
                v.memset(WROW[:], 0.0).then_inc(decay_row, 1)
                dve.wait_ge(decay_row, 1)
                v.tensor_scalar(WROW[:], WROW[:], WDEC[:], None, ALU.add).then_inc(decay_row, 1)
                dve.wait_ge(decay_row, 2)

            each_iteration(dve, iteration, after_first=decay_along_tokens, dma_counts=(1, -1, -3))

        @block.scalar
        def _(act):
            a = nc.scalar

            @step
            def normed(b, n, src, dst, dst_ready, dst_used):
                act.wait_ge(n.nb_ready, b.done)
                for s in dst_used:
                    if b.later:
                        act.wait_ge(s, b.before)
                for j in range(J):
                    last = a.activation(dst[:, j, :], src[:, j, :], ACT.Identity, scale=n.rs[:, j:j + 1], bias=n.nb[:, j:j + 1])
                last.then_inc(dst_ready, 1)

            @step
            def evacuate(b, src, src_ready, dst, dst_ready, dst_used):
                act.wait_ge(src_ready, b.done)
                for s in dst_used:
                    if b.later:
                        act.wait_ge(s, b.before)
                a.activation(dst, src, ACT.Copy).then_inc(dst_ready, 1)

            @step
            def evacuate_affine(b, src_ready, bank, dst, gain, shift, dst_ready, dst_used):
                act.wait_ge(src_ready, b.done)
                for s in dst_used:
                    if b.later:
                        act.wait_ge(s, b.before)
                a.activation(dst[:, 1:], bank[:], ACT.Identity, scale=vec(gain), bias=vec(shift)).then_inc(dst_ready, 1)

            @step
            def ffn_y_bias(b, f):
                act.wait_ge(f.yT_psum, b.done)
                if b.later:
                    act.wait_ge(f.z_psum, b.before)
                a.activation(f.yTb[:], f.bank_T[:], ACT.Identity, bias=vec("b2")).then_inc(f.yTb_ready, 1)

            @step
            def ffn_relu(b, f, n):
                if b.first:
                    act.wait_ge(loaded["ffn"], 5 * DMA)
                act.wait_ge(f.h_psum[n], b.done)
                if b.later:
                    act.wait_ge(f.z_psum, b.before)
                a.activation(f.h[:, n, :], f.bank_h[n][:], ACT.Relu, bias=B1[:, n:n + 1]).then_inc(f.h_ready[n], 1)

            @step
            def exp_low(b):
                act.wait_ge(low_ready, b.done)
                if b.later:
                    act.wait_ge(nd_ready, b.before)
                a.activation(EA[:, 0:3:2, :], LOW[:], ACT.Exp).then_inc(ea_ready, 1)

            @step
            def exp_high(b):
                act.wait_ge(high_ready, b.done)
                if b.later:
                    act.wait_ge(m1_ready, b.before)
                a.activation(EB[:], HIGH[:], ACT.Exp, scale=-1.0).then_inc(eb_ready, 1)

            @step
            def one(b, dst, src, func, src_ready, dst_ready, dst_used, **more):
                act.wait_ge(src_ready, b.done)
                if b.later:
                    act.wait_ge(dst_used, b.before)
                a.activation(dst[:], src[:], func, **more).then_inc(dst_ready, 1)

            @step
            def cmix_relu(b, n):
                act.wait_ge(kk_psum[n], b.done)
                if b.later:
                    act.wait_ge(kk_ready[n], b.before)
                a.activation(KR[:, n, :], bank_kk[n][:], ACT.Relu).then_inc(kr_ready[n], 1)

            @step
            def cmix_square(b, n):
                act.wait_ge(kr_ready[n], b.done)
                if b.later:
                    act.wait_ge(kv_psum, b.before)
                a.activation(KK[:, n, :], KR[:, n, :], ACT.Square).then_inc(kk_ready[n], 1)

            def iteration(s0, s1, s2, s3):
                cmix_square(s3, 2)
                cmix_square(s3, 3)
                one(s3, SG, RL2, ACT.Exp, rl2_ready, sg_ready, kvs_ready)
                normed(s1, f1.norm, X1, f1.y, f1.y_ready, [f1.yT_psum])
                exp_low(s2)
                evacuate(s1, f1.bank_T[:], f1.yT_psum, f1.yT[:], f1.yT_ready, [f1.h_psum[H - 1]])
                exp_high(s2)
                one(s2, AR, bank_r, ACT.Abs, r_psum, ar_ready, er_ready)
                ffn_y_bias(s1, f1)
                ffn_relu(s1, f1, 0)
                ffn_relu(s1, f1, 1)
                one(s2, ER, AR, ACT.Exp, ar_ready, er_ready, dn_ready, scale=-1.0)
                ffn_relu(s1, f1, 2)
                normed(s3, f2.norm, X3, f2.y, f2.y_ready, [f2.yT_psum])
                ffn_relu(s1, f1, 3)
                one(s2, LD, DN, ACT.Ln, dn_ready, ld_ready, rl_ready)
                evacuate(s3, f2.bank_T[:], f2.yT_psum, f2.yT[:], f2.yT_ready, [f2.h_psum[H - 1]])
                one(s2, RC, RL, ACT.Exp, rl_ready, rc_ready, rw_ready)
                ffn_y_bias(s3, f2)
                ffn_relu(s3, f2, 2)
                normed(s0, na, X0, XN, xn_ready, [xnT_psum, gram_psum])
                ffn_relu(s3, f2, 0)
                ffn_relu(s3, f2, 1)
                evacuate(s0, bank_aG[:, 0:C], gram_psum, GRAM[:], gram_ready, [proj_psum])
                evacuate(s0, bank_aT[:], xnT_psum, XNT[:], xnT_ready, [attn_psum])
                evacuate(s0, bank_aP[:, 0:C], proj_psum, PROJ[:], proj_ready, [attn_psum])
                normed(s2, ncm, U1, NC, nc_ready, [ncT_psum])
                ffn_relu(s3, f2, 3)
                evacuate_affine(s2, ncT_psum, bank_cT, XC, "ln2_g", "ln2_b", xc_ready, [xk2_ready, xr2_ready])
                normed(s1, nt, X2, N, n_ready, [nT_psum, u1_ready])
                one(s2, AR2, bank_r2, ACT.Abs, r2_psum, ar2_ready, er2_ready)
                evacuate_affine(s1, nT_psum, bank_tT, XA, "ln1_g", "ln1_b", xa_ready, [xk_ready, xv_ready, xr_ready])
                one(s2, ER2, AR2, ACT.Exp, ar2_ready, er2_ready, ld2_ready, scale=-1.0)
                cmix_relu(s2, 1)
                cmix_relu(s2, 0)
                one(s2, LD2, ER2, ACT.Ln, er2_ready, ld2_ready, rl2_ready, bias=ONE[:])
                cmix_square(s2, 0)
                cmix_relu(s2, 2)
                cmix_square(s2, 1)
                cmix_relu(s2, 3)

            a.preload_act_table_set("natural_log_exp_and_others")
            act.wait_ge(loaded["first"], 2 * DMA)
            a.activation(WEXP[:], vec("decay"), ACT.Exp).then_inc(decay_exp, 1)
            act.wait_ge(decay_exp, 1)
            a.mul(WDEC[:], WEXP[:], -1.0).then_inc(decay_ready, 1)
            act.wait_ge(const_ready, 5)
            act.wait_ge(pads_ready, 4)
            each_iteration(act, iteration)

        @block.tensor
        def _(pe):
            t_ = nc.tensor

            def warm_up(b, norm, bank):
                if b.quiet:
                    pe.wait_ge(norm.mv_ready, b.done)
                    for _ in range(WARM_UP):
                        t_.transpose(bank[:, 0:P], IDENT[:], IDENT[:])

            def transposed(src, bank, done):
                for j in range(J):
                    last = t_.transpose(bank[:, j * P:(j + 1) * P], src[:, j, :], IDENT[:])
                last.then_inc(done, 1)

            @step
            def attn_transpose(b, users):
                for s, count in b.freed(users):
                    pe.wait_ge(s, count)
                warm_up(b, na, bank_aT)
                pe.wait_ge(xn_ready, b.done)
                transposed(XN, bank_aT, xnT_psum)

            @step
            def attn_gram(b, users):
                pe.wait_ge(xn_ready, b.done)
                for s, count in b.freed(users):
                    pe.wait_ge(s, count)
                for j in range(J):
                    last = t_.matmul(bank_aG[:, 0:C], XN[:, j, :], XN[:, j, :], start=(j == 0), stop=(j == J - 1))
                last.then_inc(gram_psum, 1)

            @step
            def attn_proj(b, users):
                if b.first:
                    pe.wait_ge(loaded["first"], 2 * DMA)
                pe.wait_ge(gram_ready, b.done)
                for s, count in b.freed(users):
                    pe.wait_ge(s, count)
                t_.matmul(bank_aP[:, 0:C], Wq[:], GRAM[:], start=True, stop=True).then_inc(proj_psum, 1)

            @step
            def attn_apply(b, users):
                pe.wait_ge(proj_ready, b.done)
                pe.wait_ge(xnT_ready, b.done)
                for s, count in b.freed(users):
                    pe.wait_ge(s, count)
                for j in range(J):
                    last = t_.matmul(bank_aA[:, j * C:(j + 1) * C], XNT[:, j * P:(j + 1) * P], PROJ[:], start=True, stop=True)
                last.then_inc(attn_psum, 1)

            @step
            def ffn_transpose(b, f, users):
                for s, count in b.freed(users):
                    pe.wait_ge(s, count)
                warm_up(b, f.norm, f.bank_T)
                pe.wait_ge(f.y_ready, b.done)
                transposed(f.y, f.bank_T, f.yT_psum)

            @step
            def ffn_hidden(b, f, n, users):
                if b.first:
                    pe.wait_ge(loaded["ffn"], 5 * DMA)
                pe.wait_ge(f.yT_ready, b.done)
                for s, count in b.freed(users):
                    pe.wait_ge(s, count)
                t_.matmul(f.bank_h[n][:], W1[:, n * P:(n + 1) * P], f.yT[:], start=True, stop=True).then_inc(f.h_psum[n], 1)

            @step
            def ffn_start(b, f, users):
                pe.wait_ge(f.yTb_ready, b.done)
                for s, count in b.freed(users):
                    pe.wait_ge(s, count)
                for j in range(J):
                    t_.matmul(f.bank_z[:, j * C:(j + 1) * C], f.yTb[:, j * P:(j + 1) * P], IDENT[:], start=(j == 0), stop=False,
                              is_transpose=True, skip_group_check=True)

            @step
            def ffn_down(b, f, n):
                if b.first:
                    pe.wait_ge(loaded["ffn"], 5 * DMA)
                pe.wait_ge(f.h_ready[n], b.done)
                for j in range(J):
                    last = t_.matmul(f.bank_z[:, j * C:(j + 1) * C], f.h[:, n, j * P:(j + 1) * P], W2[:, n, :], start=False,
                                     stop=(n == H - 1), skip_group_check=True)
                if n == H - 1:
                    last.then_inc(f.z_psum, 1)

            @step
            def tmix_transpose(b, users):
                for s, count in b.freed(users):
                    pe.wait_ge(s, count)
                warm_up(b, nt, bank_tT)
                pe.wait_ge(n_ready, b.done)
                transposed(N, bank_tT, nT_psum)

            @step
            def tmix_product(b, x, x_ready, w, bank, done, users):
                if b.first:
                    pe.wait_ge(loaded["tmix"], 4 * DMA)
                pe.wait_ge(x_ready, b.done)
                for s, count in b.freed(users):
                    pe.wait_ge(s, count)
                t_.matmul(bank[:], w[:], x[:], start=True, stop=True).then_inc(done, 1)

            @step
            def tmix_o(b, users):
                if b.first:
                    pe.wait_ge(loaded["tmix"], 4 * DMA)
                pe.wait_ge(rw_ready, b.done)
                for s, count in b.freed(users):
                    pe.wait_ge(s, count)
                for j in range(J):
                    last = t_.matmul(bank_o[:, j * C:(j + 1) * C], RW[:, j * P:(j + 1) * P], Wo[:], start=True, stop=True)
                last.then_inc(o_psum, 1)

            @step
            def cmix_transpose(b, users):
                for s, count in b.freed(users):
                    pe.wait_ge(s, count)
                warm_up(b, ncm, bank_cT)
                pe.wait_ge(nc_ready, b.done)
                transposed(NC, bank_cT, ncT_psum)

            @step
            def cmix_up(b, n, users):
                if b.first:
                    pe.wait_ge(loaded["cmix"], 3 * DMA)
                pe.wait_ge(xk2_ready, b.done)
                for s, count in b.freed(users):
                    pe.wait_ge(s, count)
                t_.matmul(bank_kk[n][:], FWk[:, n * P:(n + 1) * P], XK2[:], start=True, stop=True).then_inc(kk_psum[n], 1)

            @step
            def cmix_down(b, n, users=()):
                if b.first:
                    pe.wait_ge(loaded["cmix"], 3 * DMA)
                pe.wait_ge(kk_ready[n], b.done)
                for s, count in b.freed(users):
                    pe.wait_ge(s, count)
                for j in range(J):
                    last = t_.matmul(bank_kv[:, j * C:(j + 1) * C], KK[:, n, j * P:(j + 1) * P], FWv[:, n, :],
                                     start=(n == 0 and j == 0), stop=(n == H - 1), skip_group_check=True)
                if n == H - 1:
                    last.then_inc(kv_psum, 1)

            @step
            def cmix_r(b, users):
                if b.first:
                    pe.wait_ge(loaded["cmix"], 3 * DMA)
                pe.wait_ge(xr2_ready, b.done)
                for s, count in b.freed(users):
                    pe.wait_ge(s, count)
                for j in range(J):
                    last = t_.matmul(bank_r2[:, j * C:(j + 1) * C], XR2[:, j * P:(j + 1) * P], FWr[:], start=True, stop=True)
                last.then_inc(r2_psum, 1)

            def iteration(s0, s1, s2, s3):
                cmix_down(s3, 1)
                cmix_down(s3, 2)
                cmix_down(s3, 3)
                tmix_product(s2, XR, xr_ready, Wr, bank_r, r_psum,
                             [(kr_ready[0], s2.before), (x1_ready, s0.before), (proj_ready, s0.before), (rl_ready, s2.before)])
                ffn_transpose(s1, f1, [(kr_ready[2], s2.before), (f1.zg_ready, s1.before), (f1.yTb_ready, s1.before)])
                tmix_product(s2, XV, xv_ready, Wv, bank_v, v_psum,
                             [(xa_ready, s1.before), (f2.h_ready[1], s3.before), (f1.h_ready[3], s1.before), (m2_ready, s2.before)])
                ffn_hidden(s1, f1, 1,
                           [(diff_ready, s1.before), (kr_ready[1], s2.before), (f2.h_ready[3], s3.before), (f2.yTb_ready, s3.before), (f1.h_ready[1], s1.before)])
                ffn_hidden(s1, f1, 0,
                           [(f2.zg_ready, s3.before), (xnT_ready, s0.before), (f2.h_ready[0], s3.before), (f1.h_ready[2], s1.before), (f1.h_ready[0], s1.before)])
                ffn_start(s1, f1, [(f1.yTb_ready, s1.done), (kr_ready[2], s2.before), (f1.zg_ready, s1.before)])
                ffn_hidden(s1, f1, 2,
                           [(f1.h_ready[0], s1.done), (f2.zg_ready, s3.before), (xnT_ready, s0.before), (f2.h_ready[0], s3.before), (f1.h_ready[2], s1.before)])
                ffn_down(s1, f1, 0)
                ffn_hidden(s1, f1, 3,
                           [(m2_ready, s2.done), (xa_ready, s1.before), (f2.h_ready[1], s3.before), (f1.h_ready[3], s1.before)])
                ffn_down(s1, f1, 1)
                ffn_transpose(s3, f2,
                              [(f1.h_ready[1], s1.done), (diff_ready, s1.before), (kr_ready[1], s2.before), (f2.h_ready[3], s3.before), (f2.yTb_ready, s3.before)])
                ffn_down(s1, f1, 2)
                ffn_down(s1, f1, 3)
                ffn_hidden(s3, f2, 0,
                           [(f1.h_ready[2], s1.done), (f1.h_ready[0], s1.done), (f2.zg_ready, s3.before), (xnT_ready, s0.before), (f2.h_ready[0], s3.before)])
                ffn_hidden(s3, f2, 2, [(rl2_ready, s2.before), (f2.h_ready[2], s3.before)])
                tmix_o(s2, [(kr_ready[3], s2.before), (xc_ready, s2.before), (u1_ready, s2.before)])
                ffn_hidden(s3, f2, 3,
                           [(f2.yTb_ready, s3.done), (f1.h_ready[1], s1.done), (diff_ready, s1.before), (kr_ready[1], s2.before), (f2.h_ready[3], s3.before)])
                ffn_hidden(s3, f2, 1,
                           [(f1.h_ready[3], s1.done), (m2_ready, s2.done), (xa_ready, s1.before), (f2.h_ready[1], s3.before)])
                attn_transpose(s0,
                               [(f2.h_ready[0], s3.done), (f1.h_ready[2], s1.done), (f1.h_ready[0], s1.done), (f2.zg_ready, s3.before), (xnT_ready, s0.before)])
                attn_gram(s0, [(kvs_ready, s2.before), (gram_ready, s0.before)])
                attn_proj(s0,
                          [(rl_ready, s2.done), (kr_ready[0], s2.before), (x1_ready, s0.before), (proj_ready, s0.before)])
                ffn_start(s3, f2,
                          [(xnT_ready, s0.done), (f2.h_ready[0], s3.done), (f1.h_ready[2], s1.done), (f1.h_ready[0], s1.done), (f2.zg_ready, s3.before)])
                attn_apply(s0,
                           [(proj_ready, s0.done), (rl_ready, s2.done), (kr_ready[0], s2.before), (x1_ready, s0.before)])
                ffn_down(s3, f2, 0)
                cmix_transpose(s2, [(u1_ready, s2.done), (kr_ready[3], s2.before), (xc_ready, s2.before)])
                ffn_down(s3, f2, 1)
                ffn_down(s3, f2, 2)
                ffn_down(s3, f2, 3)
                cmix_r(s2, [(f2.h_ready[2], s3.done), (rl2_ready, s2.before)])
                tmix_transpose(s1,
                               [(f2.h_ready[1], s3.done), (f1.h_ready[3], s1.done), (m2_ready, s2.done), (xa_ready, s1.before)])
                cmix_up(s2, 1,
                        [(f2.h_ready[3], s3.done), (f2.yTb_ready, s3.done), (f1.h_ready[1], s1.done), (diff_ready, s1.before), (kr_ready[1], s2.before)])
                cmix_up(s2, 0,
                        [(x1_ready, s0.done), (proj_ready, s0.done), (rl_ready, s2.done), (kr_ready[0], s2.before)])
                cmix_up(s2, 2, [(f1.zg_ready, s1.done), (f1.yTb_ready, s1.done), (kr_ready[2], s2.before)])
                cmix_up(s2, 3, [(xc_ready, s2.done), (u1_ready, s2.done), (kr_ready[3], s2.before)])
                tmix_product(s1, XK, xk_ready, Wk, bank_k, k_psum,
                             [(kr_ready[1], s2.done), (f2.h_ready[3], s3.done), (f2.yTb_ready, s3.done), (f1.h_ready[1], s1.done), (diff_ready, s1.before)])
                cmix_down(s2, 0, [(gram_ready, s0.done), (kvs_ready, s2.before)])

            pe.wait_ge(ident_ready, 1)
            each_iteration(pe, iteration)


def kernel(**inputs):
    import numpy as np
    import concourse.bacc as bacc
    from concourse.bass_utils import run_bass_kernel_spmd

    get = {n: np.asarray(a) for n, a in inputs.items()}
    rw = {n[len("L0_attn_b_"):]: a for n, a in get.items() if n.startswith("L0_attn_b_")}
    ffn = {n[len("L0_ffn_"):]: a for n, a in get.items() if n.startswith("L0_ffn_")}
    hidden = get["L0_attn_a_hidden_states"]
    C = hidden.shape[2]
    J = hidden.shape[1] // P
    vectors = {"ln1_g": rw["ln1_g"], "ln1_b": rw["ln1_b"], "ln2_g": rw["ln2_g"], "ln2_b": rw["ln2_b"],
               "decay": rw["time_decay"], "first": rw["time_first"], "mix_k": rw["time_mix_k"],
               "mix_v": rw["time_mix_v"], "mix_r": rw["time_mix_r"], "cm_k": rw["cm_k"], "cm_r": rw["cm_r"],
               "b2": ffn["b2"][0]}
    laid = {
        "hidden": hidden, "w_q": get["L0_attn_a_W_q"],
        "w1": ffn["w1"][0], "w2": ffn["w2"][0], "b1": ffn["b1"][0].reshape(-1, P).T,
        "wk": rw["att_Wk"].T, "wv": rw["att_Wv"].T, "wr": rw["att_Wr"].T, "wo": rw["att_Wo"].T,
        "f_wk": rw["ffn_Wk"].T, "f_wr": rw["ffn_Wr"].T, "f_wv": rw["ffn_Wv"].T,
        "vectors": np.stack([vectors[n] for n in VECTORS], axis=1),
        "gamma": np.tile(ffn["gamma"], (P, 1)), "beta": np.tile(ffn["beta"], (P, J)),
    }
    nc = bacc.Bacc("TRN2", target_bir_lowering=False, num_devices=1)
    arrays, args = {}, []
    for name, a in laid.items():
        a = np.ascontiguousarray(a)
        arrays["in_" + name] = a
        args.append(nc.dram_tensor("in_" + name, a.shape, mybir.dt.from_np(a.dtype), kind="ExternalInput").ap())
    args.append(nc.dram_tensor("out_x", hidden.shape, F32, kind="ExternalOutput").ap())
    hybrid_layer(nc, *args)
    return run_bass_kernel_spmd(nc, [arrays], core_ids=[0]).results[0]["out_x"]
```
